# Optimizing a Trainium2 kernel written in Bass

```python
import numpy as np
import jax
import jax.numpy as jnp

def _softmax(x, axis=-1):
    return jax.nn.softmax(x, axis=axis)

def _gelu(x):
    return jax.nn.gelu(x, approximate=True)

def _silu(x):
    return jax.nn.silu(x)

def _sigmoid(x):
    return jax.nn.sigmoid(x)

def _layernorm(x, axis=-1, eps=1e-05):
    m = jnp.mean(x, axis=axis, keepdims=True)
    v = jnp.var(x, axis=axis, keepdims=True)
    return (x - m) / jnp.sqrt(v + eps)

def _scatter_add(tgt, idx, src, axis=0):
    return tgt.at[idx].add(src)

def _segment_sum(src, seg, n):
    return jax.ops.segment_sum(src, seg, n)
kernel_name = 'mk_prb_d1_jaxref_r8_79e585'

def setup_inputs(seed: int=0):
    np.random.seed(seed)
    _w = jnp.asarray

    def _L0_attn_setup():
        import jax, jax.numpy as jnp
        import numpy as np
        B, S, E, H, D = (1, 256, 128, 16, 64)
        LAM_INIT = 0.8
        LN_EPS = 1e-05
        key = jax.random.key(seed)
        ks = jax.random.split(key, 6)
        w = 0.02
        return {'X': jax.random.normal(ks[0], (B, S, E), dtype=jnp.float32), 'Wq': jax.random.normal(ks[1], (H, E, 2 * D), dtype=jnp.float32) * w, 'bq': jnp.zeros((H, 2 * D), dtype=jnp.float32), 'Wk': jax.random.normal(ks[2], (H, E, 2 * D), dtype=jnp.float32) * w, 'bk': jnp.zeros((H, 2 * D), dtype=jnp.float32), 'Wv': jax.random.normal(ks[3], (H, E, D), dtype=jnp.float32) * w, 'bv': jnp.zeros((H, D), dtype=jnp.float32), 'Wo': jax.random.normal(ks[4], (H * D, E), dtype=jnp.float32) * w, 'bo': jnp.zeros((E,), dtype=jnp.float32), 'gamma': jnp.ones((E,), dtype=jnp.float32), 'beta': jnp.zeros((E,), dtype=jnp.float32), 'lam': jnp.float32(0.5)}
    _L0_attn_in = _L0_attn_setup()

    def _L0_ffn_setup():
        import jax, jax.numpy as jnp
        import numpy as np
        from jax import lax
        B, N, D, H, E, K = (16, 128, 128, 512, 8, 2)
        key = jax.random.key(seed)
        ks = jax.random.split(key, 12)
        s = 0.02
        return {'x': jax.random.normal(ks[0], (B, N, D), jnp.float32), 'alpha': jnp.asarray(0.9, jnp.float32), 'w_gate': jax.random.normal(ks[1], (D, E), jnp.float32) * s, 'b_gate': jnp.zeros((E,), jnp.float32), 'W1m': jax.random.normal(ks[2], (D, H), jnp.float32) * s, 'b1m': jnp.zeros((H,), jnp.float32), 'W2m': jax.random.normal(ks[3], (H, D), jnp.float32) * s, 'b2m': jnp.zeros((D,), jnp.float32), 'W1e': jax.random.normal(ks[4], (E, D, H), jnp.float32) * s, 'b1e': jnp.zeros((E, H), jnp.float32), 'W2e': jax.random.normal(ks[5], (E, H, D), jnp.float32) * s, 'b2e': jnp.zeros((E, D), jnp.float32)}
    _L0_ffn_in = _L0_ffn_setup()
    _d = {'L0_attn_X': _L0_attn_in['X'], 'L0_attn_Wq': _L0_attn_in['Wq'], 'L0_attn_bq': _L0_attn_in['bq'], 'L0_attn_Wk': _L0_attn_in['Wk'], 'L0_attn_bk': _L0_attn_in['bk'], 'L0_attn_Wv': _L0_attn_in['Wv'], 'L0_attn_bv': _L0_attn_in['bv'], 'L0_attn_Wo': _L0_attn_in['Wo'], 'L0_attn_bo': _L0_attn_in['bo'], 'L0_attn_gamma': _L0_attn_in['gamma'], 'L0_attn_beta': _L0_attn_in['beta'], 'L0_attn_lam': _L0_attn_in['lam'], 'L0_ffn_alpha': _L0_ffn_in['alpha'], 'L0_ffn_w_gate': _L0_ffn_in['w_gate'], 'L0_ffn_b_gate': _L0_ffn_in['b_gate'], 'L0_ffn_W1m': _L0_ffn_in['W1m'], 'L0_ffn_b1m': _L0_ffn_in['b1m'], 'L0_ffn_W2m': _L0_ffn_in['W2m'], 'L0_ffn_b2m': _L0_ffn_in['b2m'], 'L0_ffn_W1e': _L0_ffn_in['W1e'], 'L0_ffn_b1e': _L0_ffn_in['b1e'], 'L0_ffn_W2e': _L0_ffn_in['W2e'], 'L0_ffn_b2e': _L0_ffn_in['b2e']}
    _x0 = _d['L0_attn_X']
    _d['L0_attn_X'] = jax.random.normal(jax.random.fold_in(jax.random.key(seed), 1), (2, 1024, 128), dtype=_x0.dtype)
    del _x0
    return _d

def reference(L0_attn_X, L0_attn_Wq, L0_attn_bq, L0_attn_Wk, L0_attn_bk, L0_attn_Wv, L0_attn_bv, L0_attn_Wo, L0_attn_bo, L0_attn_gamma, L0_attn_beta, L0_attn_lam, L0_ffn_alpha, L0_ffn_w_gate, L0_ffn_b_gate, L0_ffn_W1m, L0_ffn_b1m, L0_ffn_W2m, L0_ffn_b2m, L0_ffn_W1e, L0_ffn_b1e, L0_ffn_W2e, L0_ffn_b2e):

    def _L0_attn_ref(X, Wq, bq, Wk, bk, Wv, bv, Wo, bo, gamma, beta, lam):
        import jax, jax.numpy as jnp
        import numpy as np
        B, S, E, H, D = (1, 256, 128, 16, 64)
        LAM_INIT = 0.8
        LN_EPS = 1e-05
        Q = jnp.einsum('bse,hec->bhsc', X, Wq) + bq[None, :, None, :]
        K = jnp.einsum('bse,hec->bhsc', X, Wk) + bk[None, :, None, :]
        V = jnp.einsum('bse,hed->bhsd', X, Wv) + bv[None, :, None, :]
        d = Wv.shape[-1]
        Q1, Q2 = (Q[..., :d], Q[..., d:])
        K1, K2 = (K[..., :d], K[..., d:])
        s = 1.0 / jnp.sqrt(jnp.float32(d))
        A1 = jnp.einsum('bhqd,bhkd->bhqk', Q1, K1) * s
        A2 = jnp.einsum('bhqd,bhkd->bhqk', Q2, K2) * s
        P = jax.nn.softmax(A1, axis=-1) - lam * jax.nn.softmax(A2, axis=-1)
        O = jnp.einsum('bhqk,bhkd->bhqd', P, V)
        Ocat = jnp.transpose(O, (0, 2, 1, 3)).reshape(O.shape[0], O.shape[2], -1)
        Y = Ocat @ Wo + bo
        mu = jnp.mean(Y, axis=-1, keepdims=True)
        var = jnp.var(Y, axis=-1, keepdims=True)
        Yn = (Y - mu) * jax.lax.rsqrt(var + LN_EPS) * gamma + beta
        return Yn * (1.0 - LAM_INIT)

    def _L0_ffn_ref(x, alpha, w_gate, b_gate, W1m, b1m, W2m, b2m, W1e, b1e, W2e, b2e):
        import jax, jax.numpy as jnp
        import numpy as np
        from jax import lax
        B, N, D, H, E, K = (16, 128, 128, 512, 8, 2)
        main = jax.nn.gelu(x @ W1m + b1m) @ W2m + b2m
        logits = jnp.mean(x, axis=1) @ w_gate + b_gate
        probs = jax.nn.softmax(logits, axis=-1)
        top_vals, top_idx = lax.top_k(probs, K)
        gate_w = top_vals / jnp.sum(top_vals, axis=-1, keepdims=True)
        W1g = W1e[top_idx]
        b1g = b1e[top_idx]
        W2g = W2e[top_idx]
        b2g = b2e[top_idx]
        h = jax.nn.gelu(jnp.einsum('bnd,bkdh->bknh', x, W1g) + b1g[:, :, None, :])
        eo = jnp.einsum('bknh,bkhd->bknd', h, W2g) + b2g[:, :, None, :]
        expert_out = jnp.einsum('bk,bknd->bnd', gate_w, eo)
        a = jnp.clip(alpha, 0.1, 1.0)
        return a * main + (1.0 - a) * expert_out
    x = L0_attn_X
    xn = _layernorm(x, axis=-1)
    x = x + _L0_attn_ref(xn, L0_attn_Wq, L0_attn_bq, L0_attn_Wk, L0_attn_bk, L0_attn_Wv, L0_attn_bv, L0_attn_Wo, L0_attn_bo, L0_attn_gamma, L0_attn_beta, L0_attn_lam) + _L0_ffn_ref(xn, L0_ffn_alpha, L0_ffn_w_gate, L0_ffn_b_gate, L0_ffn_W1m, L0_ffn_b1m, L0_ffn_W2m, L0_ffn_b2m, L0_ffn_W1e, L0_ffn_b1e, L0_ffn_W2e, L0_ffn_b2e)
    return x

_drawn_inputs = setup_inputs


def setup_inputs(seed=0):
    import zlib

    import numpy as np

    out = dict(_drawn_inputs(seed))
    spreads = {'L0_attn_bq': (0.0, 0.8),
     'L0_attn_bk': (0.0, 2.0),
     'L0_attn_bv': (0.0, 0.74),
     'L0_attn_bo': (0.0, 0.282),
     'L0_attn_gamma': (1.0, 0.2),
     'L0_attn_beta': (0.0, 0.471),
     'L0_ffn_b_gate': (0.0, 0.763),
     'L0_ffn_b1m': (0.0, 0.404),
     'L0_ffn_b2m': (0.0, 0.1),
     'L0_ffn_b1e': (0.0, 0.8),
     'L0_ffn_b2e': (0.0, 0.8)}
    factors = {'L0_attn_Wq': 8.0,
     'L0_attn_Wk': 8.0,
     'L0_attn_Wv': 8.0,
     'L0_ffn_w_gate': 8.0,
     'L0_ffn_W1e': 8.0,
     'L0_ffn_W2e': 8.0}
    for name, (base, spread) in spreads.items():
        noise = np.random.default_rng([zlib.crc32(name.encode()), seed]).standard_normal(out[name].shape)
        drawn = base * np.exp(spread * noise) if base else spread * noise
        out[name] = jnp.asarray(drawn.astype(out[name].dtype))
    for name, factor in factors.items():
        out[name] = (out[name] * factor).astype(out[name].dtype)
    return out
```

```python
from contextlib import ExitStack

import concourse.bass as bass
from concourse import mybir

F32 = mybir.dt.float32
F32R = mybir.dt.float32r
U32 = mybir.dt.uint32
ALU = mybir.AluOpType
ACT = mybir.ActivationFunctionType
AX = mybir.AxisListType

P = 128
B, S, E = 2, 1024, 128
H, D = 16, 64
TOK = B * S
NT = TOK // P
TB = S // P
IT = B * H
STEPS = IT * TB
QB = 4
KC = S // P
HID, NEXP, TOPK = 512, 8, 2
HC = HID // P
SETS = 1 + B * TOPK
LAG = 3
BANK = 512
UNITS = B * (1 + TOPK) * HC
SET_STEPS = 4 + 2 * SETS + 4 * B
BODY = 2 * TB
LN_EPS = 1e-5
OUT_SCALE = 0.2
QK_SCALE = 0.125
GELU_A, GELU_C = 0.044715, 0.7978845608028654


def build(nc, X, Wq, bq, Wk, bk, Wv, bv, Wo, bo, gamma, beta, lam,
          alpha, w_gate, b_gate, W1m, b1m, W2m, b2m, W1e, b1e, W2e, b2e, out):
    q_scratch = nc.dram_tensor("q_scratch", (IT, P, S), F32, kind="Internal").ap()
    k_scratch = nc.dram_tensor("k_scratch", (IT, P, S), F32, kind="Internal").ap()
    v_scratch = nc.dram_tensor("v_scratch", (IT, P, KC * D), F32, kind="Internal").ap()
    gate_scratch = nc.dram_tensor("gate_scratch", (1, B * TOPK), F32, kind="Internal").ap()

    with ExitStack() as ctx:
        def sb(name, cols, dt=F32):
            return ctx.enter_context(nc.sbuf_tensor(name, [P, cols], dt))

        def sem(name):
            return ctx.enter_context(nc.semaphore(name))

        x_all = sb("x_all", NT * E)
        x3 = x_all[:, :].rearrange("p (t e) -> p t e", e=E)
        xT_hi = sb("xT_hi", TOK, F32R)
        xT_lo = sb("xT_lo", TOK, F32R)
        y_acc = sb("y_acc", NT * E)
        y3 = y_acc[:, :].rearrange("p (t e) -> p t e", e=E)
        wo_dup = sb("wo_dup", H * E)
        wo3 = wo_dup[:, :].rearrange("p (h e) -> p h e", e=E)
        work = sb("work", 8192)
        pt = sb("pt", 8192)
        q_st = sb("q_st", 2 * 2 * S, F32R)
        k_hi = sb("k_hi", 2 * 2 * S, F32R)
        k_lo = sb("k_lo", 2 * 2 * S, F32R)
        v_h = sb("v_h", 2 * KC * D)
        p_mix = sb("p_mix", 4 * S)
        o_t = sb("o_t", 2 * BANK)
        ident = sb("ident", P)
        w1_raw = sb("w1_raw", SETS * HID)
        w2 = sb("w2", SETS * HC * E)
        bq_col = sb("bq_col", H)
        bk_col = sb("bk_col", H)
        b1_col = sb("b1_col", SETS * HC)
        b2_bc = sb("b2_bc", SETS * E)
        gb_bc = sb("gb_bc", 3 * E)
        small = sb("small", 512)
        top_idx = sb("top_idx", 8, U32)

        sum_x, mean_x, var_x = (small[:, i * NT:(i + 1) * NT] for i in range(3))
        std_x, rstd_x, tmp_x = (small[:, i * NT:(i + 1) * NT] for i in range(3, 6))
        rowsum = small[:, 96:100]
        mean_tok = small[:, 100:102]
        lam_neg = small[:, 102:103]
        a_mix = small[:, 103:104]
        a_rest = small[:, 104:105]
        coef = small[:, 105:105 + SETS]
        coef_half = small[:, 110:110 + SETS]
        gates = small[:, 116:120]
        logit, prob = small[0:B, 120:128], small[0:B, 128:136]
        lg_max, lg_sum = small[0:B, 136:137], small[0:B, 137:138]
        top8 = small[0:B, 138:146]
        gate_w = small[0:B, 146:148]
        bg_bc = small[0:B, 148:156]
        neg_max = small[:, 160:164]
        l_sum = small[:, 164:172]
        mix_c = small[:, 172:174]
        l_inv = small[:, 176:176 + 32]
        wg = small[:, 208:216]
        lam_in = small[:, 216:217]
        al_in = small[:, 217:218]
        bq_s = small[:, 224:240]
        bq_now = small[:, 240:242]
        zero = small[:, 242:243]

        raw_q, raw_k = work[:, 0:2 * S], work[:, 2 * S:4 * S]
        e2_buf = work[:, 4 * S:8 * S]
        pt4 = pt[:, :].rearrange("p (n c q) -> p n c q", n=2, c=KC)
        qs4 = q_st[:, :].rearrange("p (n s t) -> p n s t", n=2, s=2)
        kh4 = k_hi[:, :].rearrange("p (n s t) -> p n s t", n=2, s=2)
        kl4 = k_lo[:, :].rearrange("p (n s t) -> p n s t", n=2, s=2)
        vh4 = v_h[:, :].rearrange("p (n c d) -> p n c d", n=2, c=KC)
        bv_bc = o_t[:, :]
        wqk_raw = v_h[:, 0:4 * P]
        wqk_hi, wqk_lo = k_hi[:, 2 * S:2 * S + 4 * P], k_lo[:, 2 * S:2 * S + 4 * P]
        wv_raw = w1_raw[:, 0:H * D]
        wv_hi, wv_lo = k_hi[:, 0:H * D], k_lo[:, 0:H * D]
        v_st = [t[:, :].rearrange("p (h c d) -> p h c d", h=H, c=KC) for t in (pt, work)]
        qk_out = pt[:, :].rearrange("p (n w t) -> p n w t", n=2, w=2)
        w1_hi, w1_lo = q_st[:, 0:SETS * HID], k_hi[:, 0:SETS * HID]
        hidden = [pt[:, i * S:(i + 1) * S] for i in range(4)]
        z_buf = [work[:, i * S:(i + 1) * S] for i in range(2)]
        t_buf = [work[:, (2 + i) * S:(3 + i) * S] for i in range(2)]
        y_sq = p_mix[:, 0:2 * S].rearrange("p (t e) -> p t e", e=E)
        w1r3 = w1_raw[:, :].rearrange("p (s n) -> p s n", s=SETS)
        w24 = w2[:, :].rearrange("p (s c e) -> p s c e", s=SETS, c=HC)

        ps = ctx.enter_context(nc.psum_tensor("ps", [P, 8 * BANK], F32))
        slot = [ps[:, i * S:(i + 1) * S] for i in range(3)]
        pt_ps = ps[:, 6 * BANK:7 * BANK]
        o_ps = ps[:, 7 * BANK:8 * BANK]

        x_loaded = [sem(f"x_loaded{b}") for b in range(B)]
        small_loaded, bias_loaded = sem("small_loaded"), sem("bias_loaded")
        wv_loaded, wo_loaded, experts_loaded = sem("wv_loaded"), sem("wo_loaded"), sem("experts_loaded")
        id_ready, ln_step, sqrt_done = sem("id_ready"), sem("ln_step"), sem("sqrt_done")
        xn_ready, xt_ps, xt_hi, xt_lo = sem("xn_ready"), sem("xt_ps"), sem("xt_hi"), sem("xt_lo")
        wv_split, v_mm, v_evac = sem("wv_split"), sem("v_mm"), sem("v_evac")
        v_stored = [sem(f"v_stored{b}") for b in range(B)]
        route, route_mm, route_act = sem("route"), sem("route_mm"), sem("route_act")
        gates_out, gates_in, set_step = sem("gates_out"), sem("gates_in"), sem("set_step")
        bqs_ready, bq_col_ready = sem("bqs_ready"), sem("bq_col_ready")
        w_loaded = [sem(f"w_loaded{i}") for i in range(2)]
        w_split, q_mm, k_mm, q_evac, k_evac = (sem("w_split"), sem("q_mm"), sem("k_mm"), sem("q_evac"),
                                               sem("k_evac"))
        qk_stored = [sem(f"qk_stored{i}") for i in range(2)]
        raw_loaded = sem("raw_loaded")
        v_loaded = [sem(f"v_loaded{i}") for i in range(2)]
        khi_done, qhi_done, split_done = sem("khi_done"), sem("qhi_done"), sem("split_done")
        s_ready, max_done, exp_done = sem("s_ready"), sem("max_done"), sem("exp_done")
        recip_done, c_done = sem("recip_done"), sem("c_done")
        scaled, mix_done = sem("scaled"), sem("mix_done")
        pt_ready, pt_evac = sem("pt_ready"), sem("pt_evac")
        pv_done, o_evac, y_mm, y_evac = sem("pv_done"), sem("o_evac"), sem("y_mm"), sem("y_evac")
        w1_split, h_mm, z_done, g_step = sem("w1_split"), sem("h_mm"), sem("z_done"), sem("g_step")
        tanh_done, h_done, out_mm, f_out = sem("tanh_done"), sem("h_done"), sem("out_mm"), sem("f_out")
        lny, lny_pool, lny_sqrt, res_ready = sem("lny"), sem("lny_pool"), sem("lny_sqrt"), sem("res_ready")
        stored = sem("stored")

        def after(eng, s, count):
            if not isinstance(count, int) or count > 0:
                eng.wait_ge(s, count)

        def now(g, k, lag=0):
            return not isinstance(g, int) or 0 <= g * BODY + k - lag < STEPS

        def attention(eng, step, lag):
            for k in range(BODY):
                step(0, k)
            with eng.Fori(1, STEPS // BODY - 1) as g:
                for k in range(BODY):
                    step(g, k)
            for k in range(BODY):
                step(STEPS // BODY - 1, k)
            for k in range(lag):
                step(STEPS // BODY, k)

        SLOT = [k % 3 for k in range(2 * BODY)]

        def last_user(k):
            return next(d for d in range(1, 2 * BODY + 1) if SLOT[(k - d) % (2 * BODY)] == SLOT[k])

        block = ctx.enter_context(nc.Block())

        @block.sync
        def _(sp):
            xv = X.rearrange("b (t p) e -> p (b t) e", p=P)
            for b in range(B):
                sp.dma_start(x3[:, b * TB:(b + 1) * TB, :], xv[:, b * TB:(b + 1) * TB, :]).then_inc(x_loaded[b], 16)
            sp.dma_start(wv_raw.rearrange("p (h d) -> p h d", h=H), Wv.rearrange("h e d -> e h d"))\
                .then_inc(wv_loaded, 16)
            sp.dma_start(bv_bc, bv.rearrange("h d -> (h d)").partition_broadcast(P)).then_inc(bias_loaded, 16)
            for i, v in enumerate((gamma, beta, bo)):
                sp.dma_start(gb_bc[:, i * E:(i + 1) * E], v.partition_broadcast(P)).then_inc(bias_loaded, 16)
            for half in range(2):
                sp.dma_start(wo3[half * D:(half + 1) * D, :, :], Wo.rearrange("(h d) e -> d h e", d=D))\
                    .then_inc(wo_loaded, 16)

            for b in range(B):
                sp.wait_ge(v_evac, 2 * TB * (b + 1))
                sp.dma_start(v_scratch[b * H:(b + 1) * H, :, :].rearrange("h p n -> p h n"),
                             (pt, work)[b][:, :].rearrange("p (h n) -> p h n", h=H)).then_inc(v_stored[b], 16)

            def store_qk(g, par):
                h = 2 * g + par
                sp.wait_ge(q_evac, 2 * h + 2)
                sp.dma_start(q_scratch.rearrange("(b h) p t -> h p b t", b=B)[bass.ds(h, 1), :, :, :]
                             .rearrange("o p b t -> (o p) b t"),
                             qk_out[:, par, 0, :].rearrange("p (b t) -> p b t", b=B)).then_inc(qk_stored[par], 16)
                sp.wait_ge(k_evac, 2 * h + 2)
                sp.dma_start(k_scratch.rearrange("(b h) p t -> h p b t", b=B)[bass.ds(h, 1), :, :, :]
                             .rearrange("o p b t -> (o p) b t"),
                             qk_out[:, par, 1, :].rearrange("p (b t) -> p b t", b=B)).then_inc(qk_stored[par], 16)

            with sp.Fori(0, H // 2) as g:
                for par in range(2):
                    store_qk(g, par)
            for par in range(2):
                sp.wait_ge(qk_stored[par], 32 * (H // 2))
            for b in range(B):
                sp.wait_ge(v_stored[b], 16)

            def load(i, par):
                after(sp, split_done, 8 * i)
                for half in range(2):
                    rows = slice(half * D, (half + 1) * D)
                    for dst, src in ((raw_q, q_scratch), (raw_k, k_scratch)):
                        sp.dma_start(dst[rows, :].rearrange("p (s t) -> p s t", s=2),
                                     src[bass.ds(i, 1), :, :].rearrange("o (s d) t -> (o d) s t", d=D))\
                            .then_inc(raw_loaded, 16)
                after(sp, pv_done, 2 * i - 2)
                sp.dma_start(v_h[:, par * KC * D:(par + 1) * KC * D],
                             v_scratch[bass.ds(i, 1), :, :].rearrange("o p n -> (o p) n"))\
                    .then_inc(v_loaded[par], 16)

            load(0, 0)
            load(1, 1)
            with sp.Fori(1, IT // 2) as g:
                for par in range(2):
                    load(2 * g + par, par)

            ov = out.rearrange("b (t p) e -> p (b t) e", p=P)
            for i in range(NT // 4):
                sp.wait_ge(f_out, i + 1)
                sp.dma_start(ov[:, 4 * i:4 * i + 4, :], y3[:, 4 * i:4 * i + 4, :]).then_inc(stored, 16)
            sp.wait_ge(stored, 16 * NT // 4)

        @block.gpsimd
        def _(pool):
            pool.memset(ident[:, :], 0.0).then_inc(id_ready, 1)
            pool.wait_ge(id_ready, 1)
            pool.affine_select(out=ident[:, :], in_=ident[:, :], compare_op=ALU.not_equal, fill=1.0,
                               base=0, pattern=[[-1, P]], channel_multiplier=1).then_inc(id_ready, 1)
            pool.dma_start(wg, w_gate).then_inc(small_loaded, 16)
            pool.dma_start(bg_bc, b_gate.partition_broadcast(B)).then_inc(small_loaded, 16)
            pool.dma_start(lam_in, lam.partition_broadcast(P)).then_inc(small_loaded, 16)
            pool.dma_start(al_in, alpha.partition_broadcast(P)).then_inc(small_loaded, 16)

            pool.memset(zero, 0.0).then_inc(id_ready, 1)

            pool.wait_ge(wv_loaded, 16)
            pool.tensor_copy(wv_hi, wv_raw).then_inc(wv_split, 1)
            pool.wait_ge(wv_split, 1)
            pool.tensor_tensor(wv_lo, wv_raw, wv_hi.bitcast(F32), ALU.subtract).then_inc(wv_split, 1)

            def split_w(g, par, first):
                h = 2 * g + par
                sl = slice(par * 2 * P, (par + 1) * 2 * P)
                pool.wait_ge(w_loaded[par], 32 * g + 32)
                if not first:
                    pool.wait_ge(k_mm, 2 * h - 2)
                pool.tensor_tensor(wqk_hi[:, sl], wqk_raw[:, sl], zero.to_broadcast([P, 2 * P]), ALU.subtract)\
                    .then_inc(w_split, 1)
                pool.wait_ge(w_split, 2 * h + 1)
                pool.tensor_tensor(wqk_lo[:, sl], wqk_raw[:, sl], wqk_hi[:, sl].bitcast(F32), ALU.subtract)\
                    .then_inc(w_split, 1)

            pool.wait_ge(id_ready, 3)
            for par in range(2):
                split_w(0, par, True)
            with pool.Fori(1, H // 2) as g:
                for par in range(2):
                    split_w(g, par, False)

            def load_set(s_, w1, b1, w2_, b2):
                pool.dma_start(w1r3[:, s_, :], w1).then_inc(experts_loaded, 16)
                pool.dma_start(w24[:, s_, :, :], w2_.rearrange("(c p) e -> p c e", p=P)).then_inc(experts_loaded, 16)
                pool.dma_start(b1_col[:, s_ * HC:(s_ + 1) * HC], b1).then_inc(experts_loaded, 16)
                pool.dma_start(b2_bc[:, s_ * E:(s_ + 1) * E], b2.partition_broadcast(P)).then_inc(experts_loaded, 16)

            pool.wait_ge(wv_split, 2)
            load_set(0, W1m, b1m, W2m, b2m)
            pool.wait_ge(route, 15)
            pool.dma_start(gate_scratch.rearrange("o (b k) -> (o b) k", b=B), gate_w).then_inc(gates_out, 16)
            for b in range(B):
                for c in range(TOPK):
                    e = pool.value_load(top_idx[b:b + 1, c:c + 1], min_val=0, max_val=NEXP - 1)
                    load_set(1 + TOPK * b + c, W1e[bass.ds(e, 1), :, :].rearrange("o a n -> (o a) n"),
                             b1e[bass.ds(e, 1), :, :].rearrange("o p c -> (o p) c"),
                             W2e[bass.ds(e, 1), :, :].rearrange("o n e -> (o n) e"),
                             b2e[bass.ds(e, 1), :].rearrange("o n -> (o n)"))
            pool.wait_ge(gates_out, 16)
            pool.dma_start(gates, gate_scratch.rearrange("o n -> (o n)").partition_broadcast(P))\
                .then_inc(gates_in, 16)

            def split_k(i, par, quarter):
                a = quarter * BANK
                pool.wait_ge(khi_done, i + 1)
                pool.tensor_tensor(k_lo[:, par * 2 * S + a:par * 2 * S + a + BANK], raw_k[:, a:a + BANK],
                                   k_hi[:, par * 2 * S + a:par * 2 * S + a + BANK].bitcast(F32), ALU.subtract)\
                    .then_inc(split_done, 1)

            def split_q(i, par, quarter):
                a = quarter * BANK
                if quarter == 0:
                    pool.wait_ge(qhi_done, i + 1)
                low = q_st[D:P, par * 2 * S + a:par * 2 * S + a + BANK]
                pool.tensor_tensor(low, raw_q[D:P, a:a + BANK], low.bitcast(F32), ALU.subtract)\
                    .then_inc(split_done, 1)

            def split_lo(i, par, quarters, is_q):
                done = 8 * i + 4 * is_q + quarters[0]
                if is_q:
                    after(pool, mix_done, POOL_MIX[0])
                    pool.wait_ge(split_done, done)
                for q in quarters:
                    (split_q if is_q else split_k)(i, par, q)
                if is_q:
                    pool.wait_ge(split_done, done + len(quarters))

            POOL_MIX = [0]
            for is_q in (0, 1):
                split_lo(0, 0, range(4), is_q)
            pool.wait_ge(gates_in, 16)
            pool.tensor_scalar(coef[:, 1:SETS], gates, a_rest, None, ALU.mult).then_inc(set_step, 1)
            pool.tensor_copy(coef[:, 0:1], a_mix).then_inc(set_step, 1)
            pool.wait_ge(set_step, 2)
            pool.tensor_scalar(coef_half, coef, 0.5, None, ALU.mult).then_inc(set_step, 1)
            pool.tensor_scalar(gb_bc[:, 0:2 * E], gb_bc[:, 0:2 * E], OUT_SCALE, None, ALU.mult).then_inc(set_step, 1)
            pool.wait_ge(experts_loaded, 64 * SETS)
            bias = b2_bc[:, :].rearrange("p (s e) -> p s e", s=SETS)
            done = 4
            for s_ in range(SETS):
                pool.tensor_scalar(bias[:, s_, :], bias[:, s_, :], coef[:, s_:s_ + 1], None, ALU.mult)\
                    .then_inc(set_step, 1)
                done += 1
            pool.wait_ge(set_step, done)
            for b in range(B):
                first = bias[:, 1 + TOPK * b, :]
                for v in (bias[:, 2 + TOPK * b, :], bias[:, 0, :], gb_bc[:, E:2 * E]):
                    pool.tensor_tensor(first, first, v, ALU.add).then_inc(set_step, 1)
                    done += 1
                    pool.wait_ge(set_step, done)
                xb = x3[:, b * TB:(b + 1) * TB, :]
                pool.tensor_tensor(xb, xb, first.unsqueeze(1).to_broadcast([P, TB, E]), ALU.add)\
                    .then_inc(set_step, 1)
                done += 1
            for s_ in range(SETS):
                part = w2[:, s_ * HC * E:(s_ + 1) * HC * E]
                pool.tensor_scalar(part, part, coef_half[:, s_:s_ + 1], None, ALU.mult).then_inc(set_step, 1)
                done += 1
            assert done == SET_STEPS

            def step(g, k):
                n = g * BODY + k
                if now(g, k, 1):
                    e1 = p_mix[:, (k - 1) % 4 * S:((k - 1) % 4 + 1) * S]
                    e2 = e2_buf[:, (k - 1) % 4 * S:((k - 1) % 4 + 1) * S]
                    pool.wait_ge(scaled, n)
                    pool.tensor_tensor(e1, e1, e2, ALU.add).then_inc(mix_done, 1)
                if k % TB in SPLIT_AT and now(g, k, -TB):
                    is_q, quarters = SPLIT_AT[k % TB]
                    POOL_MIX[0] = n
                    split_lo(g * 2 + k // TB + 1, (k // TB + 1) % 2, quarters, is_q)

            SPLIT_AT = {1: (0, (0, 1)), 2: (0, (2, 3)), 3: (1, (0, 1)), 4: (1, (2, 3))}
            attention(pool, step, 1)

            def bc_tok(v):
                return v.unsqueeze(2).to_broadcast([P, NT, E])

            pool.wait_ge(lny, 2)
            pool.tensor_tensor(y3, y3, bc_tok(mean_x), ALU.subtract).then_inc(lny_pool, 1)
            pool.wait_ge(lny_pool, 1)
            pool.tensor_tensor(y_sq, y3, y3, ALU.mult).then_inc(lny_pool, 1)
            pool.wait_ge(lny, 8)
            pool.tensor_tensor(y3, y3, bc_tok(rstd_x), ALU.mult).then_inc(lny_pool, 1)
            pool.wait_ge(lny_pool, 3)
            pool.tensor_tensor(y3, y3, gb_bc[:, 0:E].unsqueeze(1).to_broadcast([P, NT, E]), ALU.mult)\
                .then_inc(lny_pool, 1)
            pool.wait_ge(lny_pool, 4)
            pool.tensor_tensor(y3, y3, x3, ALU.add).then_inc(res_ready, 1)

        @block.tensor
        def _(pe):
            pe.wait_ge(id_ready, 2)
            for i in range(NT):
                if i % 8 == 0:
                    pe.wait_ge(xn_ready, i // 8 + 1)
                mm = pe.transpose(ps[:, i * P:(i + 1) * P], p_mix[:, i * E:(i + 1) * E], ident[:, :])
                if i % 4 == 3:
                    mm.then_inc(xt_ps, 1)
            pe.wait_ge(wv_split, 2)
            for i in range(NT):
                for hv in range(2):
                    u = 2 * i + hv
                    bank = 4 + u % 4
                    if u % 8 == 0:
                        pe.wait_ge(xt_lo, i // 4 + 1)
                    after(pe, v_evac, u - 3)
                    for j, (a, w) in enumerate(((xT_hi, wv_hi), (xT_lo, wv_hi), (xT_hi, wv_lo))):
                        mm = pe.matmul(ps[:, bank * BANK:(bank + 1) * BANK], a[:, i * P:(i + 1) * P],
                                       w[:, hv * BANK:(hv + 1) * BANK], start=j == 0, stop=j == 2)
                    mm.then_inc(v_mm, 1)
            pe.wait_ge(route, 2)
            pe.wait_ge(small_loaded, 64)
            pe.matmul(ps[0:B, 0:NEXP], mean_tok, wg, start=True, stop=True).then_inc(route_mm, 1)

            pe.wait_ge(v_evac, 2 * NT)
            pe.wait_ge(route, 3)

            def project(g, par, first):
                h = 2 * g + par
                pe.wait_ge(w_split, 2 * h + 2)
                for w, evac, mm_sem in ((0, q_evac, q_mm), (1, k_evac, k_mm)):
                    for half in range(2):
                        if not first:
                            pe.wait_ge(evac, 2 * h - 1 + half)
                        for j, (wt, a) in enumerate(((wqk_hi, xT_hi), (wqk_lo, xT_hi), (wqk_hi, xT_lo))):
                            c0 = (par * 2 + w) * P
                            for q in range(2):
                                col = half * S + q * BANK
                                mm = pe.matmul(ps[:, w * 2 * S + col:w * 2 * S + col + BANK],
                                               wt[:, c0:c0 + P], a[:, col:col + BANK], start=j == 0, stop=j == 2)
                        mm.then_inc(mm_sem, 1)

            project(0, 0, True)
            project(0, 1, False)
            with pe.Fori(1, H // 2) as g:
                for par in range(2):
                    project(g, par, False)

            pe.wait_ge(q_evac, 2 * H)
            pe.wait_ge(k_evac, 2 * H)

            def scores(g, k, s):
                tile = 2 * k + s
                n = g * BODY + k
                after(pe, exp_done, 2 * n + s + 1 - last_user(tile))
                par, q0 = k // TB, (k % TB) * P
                for j, kk in enumerate((kh4, kl4)):
                    for half in range(2):
                        cols = slice(half * BANK, (half + 1) * BANK)
                        mm = pe.matmul(slot[SLOT[tile]][:, cols], qs4[:, par, s, q0:q0 + P], kk[:, par, s, cols],
                                       start=j == 0, stop=j == 1)
                mm.then_inc(s_ready, 1)

            def turn(g, k, half):
                n = g * BODY + k - LAG
                if half == 0:
                    pe.wait_ge(mix_done, n + 1)
                after(pe, pt_evac, 2 * n + half)
                for c in range(4):
                    col = (k - LAG) % 4 * S + (half * 4 + c) * P
                    mm = pe.transpose(pt_ps[:, c * P:(c + 1) * P], p_mix[:, col:col + P], ident[:, :])
                mm.then_inc(pt_ready, 1)

            def pv(g, kb, c0):
                blk = g * (BODY // QB) + kb
                if c0 == 0:
                    pe.wait_ge(pt_evac, 2 * QB * (blk + 1))
                    after(pe, y_evac, blk)
                    if kb % 2 == 0:
                        pe.wait_ge(v_loaded[kb // 2], 16 * (g + 1))
                for c in (c0, c0 + 1):
                    half = c % 2
                    mm = pe.matmul(o_ps[half * D:(half + 1) * D, :], vh4[:, (kb // 2) % 2, c, :],
                                   pt4[:, kb % 2, c, :], start=c < 2, stop=c >= KC - 2,
                                   skip_group_check=True)
                if c0 == KC - 2:
                    mm.then_inc(pv_done, 1)

            def out_proj(g, kb):
                head = (g * 2 + kb // 2 - 1) % H
                pe.wait_ge(o_evac, g * (BODY // QB) + kb - 1)
                for t in range(QB):
                    col = (kb % 2) * BANK + t * P
                    mm = pe.matmul(o_ps[:, t * E:(t + 1) * E], o_t[:, col:col + P],
                                   wo_dup[:, bass.ds(head * E, E)], start=True, stop=True, skip_group_check=True)
                mm.then_inc(y_mm, 1)

            def step(g, k):
                kb, j = divmod(k, QB)
                if now(g, k):
                    if k % TB == 0:
                        pe.wait_ge(split_done, 8 * (g * 2 + k // TB) + 8)
                    scores(g, k, 0)
                if now(g, k, LAG):
                    turn(g, k, 0)
                if j == 1 and now(g, k - j, 2 * QB):
                    out_proj(g, kb)
                if j == 3 and now(g, k - j, QB):
                    pv(g, kb - 1, 0)
                if j == 0 and now(g, k, 2 * QB):
                    pv(g, kb - 2, 4)
                if now(g, k):
                    scores(g, k, 1)
                if now(g, k, LAG):
                    turn(g, k, 1)
                if j == 3 and now(g, k - j, QB):
                    pv(g, kb - 1, 2)
                if j == 0 and now(g, k, 2 * QB):
                    pv(g, kb - 2, 6)

            pe.wait_ge(wo_loaded, 32)
            attention(pe, step, QB + 2)

            pe.wait_ge(w1_split, 2)

            def hidden_mm(u):
                b, i = divmod(u, (1 + TOPK) * HC)
                f, c = divmod(i, HC)
                col = (0 if f == 0 else TOPK * b + f) * HID + c * P
                after(pe, z_done, u - 1)
                for j, (w, a) in enumerate(((w1_hi, xT_hi), (w1_lo, xT_hi), (w1_hi, xT_lo))):
                    for half in range(2):
                        t0 = b * S + half * BANK
                        mm = pe.matmul(slot[u % 2][:, half * BANK:(half + 1) * BANK], w[:, col:col + P],
                                       a[:, t0:t0 + BANK], start=j == 0, stop=j == 2)
                mm.then_inc(h_mm, 1)

            def output_mm(u):
                b, i = divmod(u, (1 + TOPK) * HC)
                f, c = divmod(i, HC)
                pe.wait_ge(h_done, u + 1)
                for t in range(TB):
                    out_ps = ps[:, (4 + 2 * b) * BANK + t * E:(4 + 2 * b) * BANK + (t + 1) * E]
                    mm = pe.matmul(out_ps, hidden[u % 4][:, t * P:(t + 1) * P],
                                   w24[:, 0 if f == 0 else TOPK * b + f, c, :],
                                   start=i == 0 and t % 4 == 0, stop=i == (1 + TOPK) * HC - 1,
                                   skip_group_check=True)
                mm.then_inc(out_mm, 1)

            pe.wait_ge(y_evac, STEPS // QB)
            for u in range(UNITS + 2):
                if u < UNITS:
                    hidden_mm(u)
                if u >= 2:
                    if u == 2:
                        pe.wait_ge(set_step, SET_STEPS)
                    output_mm(u - 2)

        @block.scalar
        def _(act):
            act.dma_start(bq_col[:, :], bq).then_inc(bias_loaded, 16)
            act.dma_start(bk_col[:, :], bk).then_inc(bias_loaded, 16)

            def load_w(g, par):
                h = 2 * g + par
                for w, src in enumerate((Wq, Wk)):
                    c0 = (par * 2 + w) * P
                    act.dma_start(wqk_raw[:, c0:c0 + P],
                                  src[bass.ds(h, 1), :, :].rearrange("o e c -> (o e) c")).then_inc(w_loaded[par], 16)

            load_w(0, 0)
            load_w(0, 1)
            for b in range(B):
                act.wait_ge(ln_step, 10 * b + 6)
                act.activation(std_x[:, b * TB:(b + 1) * TB], var_x[:, b * TB:(b + 1) * TB], ACT.Sqrt)\
                    .then_inc(sqrt_done, 1)
            for i in range(NT // 4):
                act.wait_ge(xt_ps, i + 1)
                act.activation(xT_hi[:, i * BANK:(i + 1) * BANK], ps[:, i * BANK:(i + 1) * BANK], ACT.Copy,
                               accum_out=rowsum[:, i:i + 1]).then_inc(xt_hi, 1)
            act.wait_ge(bias_loaded, 96)
            act.mul(bq_s, bq_col[:, :], QK_SCALE).then_inc(bqs_ready, 1)
            act.wait_ge(bqs_ready, 1)
            act.wait_ge(route, 5)
            act.activation(prob, logit, ACT.Exp, bias=lg_max, scale=1.0, accum_out=lg_sum).then_inc(route_act, 1)

            act.wait_ge(v_stored[0], 16)

            def evac_q(g, par, first):
                h = 2 * g + par
                act.activation(bq_now[:, par:par + 1], bq_s[:, bass.ds(h, 1)], ACT.Copy).then_inc(bq_col_ready, 1)
                if not first:
                    act.wait_ge(qk_stored[par], 32 * g)
                act.wait_ge(bq_col_ready, h + 1)
                for half in range(2):
                    act.wait_ge(q_mm, 2 * h + half + 1)
                    act.activation(qk_out[:, par, 0, half * S:(half + 1) * S], ps[:, half * S:(half + 1) * S],
                                   ACT.Identity, bias=bq_now[:, par:par + 1], scale=QK_SCALE).then_inc(q_evac, 1)

            def next_w(g, par):
                act.wait_ge(w_split, 2 * (2 * g + par) + 2)
                load_w(g + 1, par)

            for par in range(2):
                next_w(0, par)
                evac_q(0, par, True)
            with act.Fori(1, H // 2 - 1) as g:
                for par in range(2):
                    next_w(g, par)
                    evac_q(g, par, False)
            for par in range(2):
                evac_q(H // 2 - 1, par, False)

            for par in range(2):
                act.wait_ge(qk_stored[par], 32 * (H // 2))
            act.wait_ge(v_stored[1], 16)

            def q_high(i, par):
                act.wait_ge(raw_loaded, 64 * (i + 1))
                after(act, s_ready, 2 * TB * (i - 1))
                act.activation(q_st[:, par * 2 * S:(par + 1) * 2 * S], raw_q, ACT.Copy).then_inc(qhi_done, 1)

            def exps(g, k, s):
                n = g * BODY + k
                act.wait_ge(max_done, 2 * n + s + 1)
                if s == 0:
                    after(act, pt_ready, 2 * (n - 3))
                else:
                    after(act, mix_done, n - 3)
                m, l = (k % 2) * 2 + s, (k % 4) * 2 + s
                act.activation((p_mix, e2_buf)[s][:, k % 4 * S:(k % 4 + 1) * S], slot[SLOT[2 * k + s]], ACT.Exp,
                               bias=neg_max[:, m:m + 1], scale=1.0, accum_out=l_sum[:, l:l + 1])\
                    .then_inc(exp_done, 1)

            def evac_pt(g, k, half):
                kb, j = divmod(k - LAG, QB)
                if half == 0 and j == 0:
                    after(act, pv_done, g * (BODY // QB) + kb - 1)
                act.wait_ge(pt_ready, 2 * (g * BODY + k - LAG) + half + 1)
                act.activation(pt4[:, kb % 2, half * 4:half * 4 + 4, j * P:(j + 1) * P],
                               pt_ps.rearrange("p (c q) -> p c q", c=4), ACT.Copy).then_inc(pt_evac, 1)

            def step(g, k):
                kb, j = divmod(k, QB)
                if j == 1 and now(g, k - j, 2 * QB):
                    act.wait_ge(pv_done, g * (BODY // QB) + kb - 1)
                    act.activation(o_t[:, (kb % 2) * BANK:(kb % 2 + 1) * BANK], o_ps, ACT.Copy).then_inc(o_evac, 1)
                if now(g, k, LAG):
                    evac_pt(g, k, 0)
                if now(g, k):
                    exps(g, k, 0)
                if now(g, k, LAG):
                    evac_pt(g, k, 1)
                if now(g, k):
                    exps(g, k, 1)
                if k % TB == 1 and now(g, k, -TB):
                    q_high(g * 2 + k // TB + 1, (k // TB + 1) % 2)

            q_high(0, 0)
            attention(act, step, QB + 2)

            for u in range(UNITS + 1):
                if u == UNITS // 3:
                    act.wait_ge(lny, 4)
                    act.activation(std_x, var_x, ACT.Sqrt).then_inc(lny_sqrt, 1)
                if u < UNITS:
                    b, i = divmod(u, (1 + TOPK) * HC)
                    f, c = divmod(i, HC)
                    col = (0 if f == 0 else TOPK * b + f) * HC + c
                    if u == 0:
                        act.wait_ge(set_step, SET_STEPS)
                    act.wait_ge(h_mm, u + 1)
                    after(act, h_done, u - 1)
                    act.activation(z_buf[u % 2], slot[u % 2], ACT.Identity, bias=b1_col[:, col:col + 1], scale=1.0)
                    act.activation(t_buf[u % 2], slot[u % 2], ACT.Square, bias=b1_col[:, col:col + 1], scale=1.0)\
                        .then_inc(z_done, 1)
                if u >= 1:
                    act.wait_ge(g_step, 2 * u)
                    act.activation(t_buf[(u - 1) % 2], t_buf[(u - 1) % 2], ACT.Tanh, scale=GELU_C)\
                        .then_inc(tanh_done, 1)

        @block.vector
        def _(dve):
            xn3 = p_mix[:, 0:2 * S].rearrange("p (t e) -> p t e", e=E)
            sq3 = work[:, 0:S].rearrange("p (t e) -> p t e", e=E)

            def inv_std(t, s, base):
                dve.reciprocal(rstd_x[:, t], std_x[:, t]).then_inc(s, 1)
                dve.wait_ge(s, base + 1)
                dve.tensor_tensor(tmp_x[:, t], rstd_x[:, t], rstd_x[:, t], ALU.mult).then_inc(s, 1)
                dve.wait_ge(s, base + 2)
                dve.scalar_tensor_tensor(out=tmp_x[:, t], in0=tmp_x[:, t], scalar=-0.5, in1=var_x[:, t],
                                         op0=ALU.mult, op1=ALU.mult).then_inc(s, 1)
                dve.wait_ge(s, base + 3)
                dve.scalar_tensor_tensor(out=rstd_x[:, t], in0=tmp_x[:, t], scalar=1.5, in1=rstd_x[:, t],
                                         op0=ALU.add, op1=ALU.mult).then_inc(s, 1)

            for b in range(B):
                t = slice(b * TB, (b + 1) * TB)
                o = 10 * b
                dve.wait_ge(x_loaded[b], 16)
                dve.tensor_reduce(sum_x[:, t], x3[:, t, :], AX.X, ALU.add).then_inc(ln_step, 1)
                dve.wait_ge(ln_step, o + 1)
                dve.tensor_scalar(mean_x[:, t], sum_x[:, t], 1.0 / E, None, ALU.mult).then_inc(ln_step, 1)
                dve.wait_ge(ln_step, o + 2)
                dve.tensor_tensor(xn3[:, t, :], x3[:, t, :],
                                  mean_x[:, t].unsqueeze(2).to_broadcast([P, TB, E]), ALU.subtract)\
                    .then_inc(ln_step, 1)
                dve.wait_ge(ln_step, o + 3)
                dve.tensor_tensor(sq3, xn3[:, t, :], xn3[:, t, :], ALU.mult).then_inc(ln_step, 1)
                dve.wait_ge(ln_step, o + 4)
                dve.tensor_reduce(sum_x[:, t], sq3, AX.X, ALU.add).then_inc(ln_step, 1)
                dve.wait_ge(ln_step, o + 5)
                dve.tensor_scalar(var_x[:, t], sum_x[:, t], 1.0 / E, LN_EPS, ALU.mult, ALU.add)\
                    .then_inc(ln_step, 1)
                dve.wait_ge(sqrt_done, b + 1)
                inv_std(t, ln_step, o + 6)
                dve.wait_ge(ln_step, o + 10)
                dve.tensor_tensor(xn3[:, t, :], xn3[:, t, :],
                                  rstd_x[:, t].unsqueeze(2).to_broadcast([P, TB, E]), ALU.mult)\
                    .then_inc(xn_ready, 1)
            for i in range(NT // 4):
                dve.wait_ge(xt_hi, i + 1)
                dve.tensor_tensor(xT_lo[:, i * BANK:(i + 1) * BANK], ps[:, i * BANK:(i + 1) * BANK],
                                  xT_hi[:, i * BANK:(i + 1) * BANK].bitcast(F32), ALU.subtract).then_inc(xt_lo, 1)
            dve.tensor_tensor(mean_tok, rowsum[:, 0:4:2], rowsum[:, 1:4:2], ALU.add).then_inc(route, 1)
            dve.wait_ge(route, 1)
            dve.tensor_scalar(mean_tok, mean_tok, 1.0 / S, None, ALU.mult).then_inc(route, 1)

            dve.wait_ge(bias_loaded, 96)
            bv3 = bv_bc.rearrange("p (h d) -> p h d", d=D)
            for u in range(2 * NT):
                i, hv = divmod(u, 2)
                bank = 4 + u % 4
                dve.wait_ge(v_mm, u + 1)
                dve.tensor_tensor(v_st[i // TB][:, hv * 8:(hv + 1) * 8, i % TB, :],
                                  ps[:, bank * BANK:(bank + 1) * BANK].rearrange("p (h d) -> p h d", d=D),
                                  bv3[:, hv * 8:(hv + 1) * 8, :], ALU.add).then_inc(v_evac, 1)

            dve.wait_ge(route_mm, 1)
            dve.tensor_tensor(logit, ps[0:B, 0:NEXP], bg_bc, ALU.add).then_inc(route, 1)
            dve.wait_ge(route, 3)
            dve.tensor_reduce(lg_max, logit, AX.X, ALU.max, negate=True).then_inc(route, 1)
            dve.tensor_scalar(a_mix, al_in, 0.1, 1.0, ALU.max, ALU.min).then_inc(route, 1)
            dve.wait_ge(route_act, 1)
            dve.reciprocal(lg_sum, lg_sum).then_inc(route, 1)
            dve.wait_ge(route, 6)
            dve.tensor_scalar(prob, prob, lg_sum, None, ALU.mult).then_inc(route, 1)
            dve.wait_ge(route, 7)
            dve.max(top8, prob).then_inc(route, 1)
            dve.wait_ge(route, 8)
            dve.max_index(top_idx[0:B, :], top8, prob).then_inc(route, 1)
            dve.tensor_tensor(lg_sum, top8[:, 0:1], top8[:, 1:2], ALU.add).then_inc(route, 1)
            dve.wait_ge(route, 10)
            dve.reciprocal(lg_sum, lg_sum).then_inc(route, 1)
            dve.wait_ge(route, 11)
            dve.tensor_scalar(gate_w, top8[:, 0:TOPK], lg_sum, None, ALU.mult).then_inc(route, 1)
            dve.tensor_scalar(lam_neg, lam_in, -1.0, None, ALU.mult).then_inc(route, 1)
            dve.tensor_scalar(a_rest, a_mix, -1.0, 1.0, ALU.mult, ALU.add).then_inc(route, 1)
            dve.tensor_copy(y3, gb_bc[:, 2 * E:3 * E].unsqueeze(1).to_broadcast([P, NT, E])).then_inc(route, 1)

            dve.wait_ge(v_stored[0], 16)

            def evac_k(g, par, first):
                h = 2 * g + par
                if not first:
                    dve.wait_ge(qk_stored[par], 32 * g)
                for half in range(2):
                    dve.wait_ge(k_mm, 2 * h + half + 1)
                    dve.tensor_scalar(qk_out[:, par, 1, half * S:(half + 1) * S],
                                      ps[:, 2 * S + half * S:2 * S + (half + 1) * S],
                                      bk_col[:, bass.ds(h, 1)], None, ALU.add).then_inc(k_evac, 1)

            for par in range(2):
                evac_k(0, par, True)
            with dve.Fori(1, H // 2) as g:
                for par in range(2):
                    evac_k(g, par, False)

            def k_high(i, par):
                dve.wait_ge(raw_loaded, 64 * (i + 1))
                after(dve, s_ready, 2 * TB * (i - 1))
                dve.tensor_copy(k_hi[:, par * 2 * S:(par + 1) * 2 * S], raw_k).then_inc(khi_done, 1)

            def row_max(g, k, s):
                m = (k % 2) * 2 + s
                dve.wait_ge(s_ready, 2 * (g * BODY + k) + s + 1)
                dve.tensor_reduce(neg_max[:, m:m + 1], slot[SLOT[2 * k + s]], AX.X, ALU.max, negate=True)\
                    .then_inc(max_done, 1)

            def step(g, k):
                kb, j = divmod(k, QB)
                m, km = g * BODY + k - 1, (k - 1) % BODY
                l, r, e = (km % 4) * 2, km * 2, km % 2
                if now(g, k):
                    row_max(g, k, 0)
                if now(g, k, 1):
                    dve.wait_ge(exp_done, 2 * m + 2)
                    dve.reciprocal(l_inv[:, r:r + 2], l_sum[:, l:l + 2]).then_inc(recip_done, 1)
                    dve.wait_ge(recip_done, m + 1)
                    dve.scalar_tensor_tensor(out=mix_c[:, e:e + 1], in0=l_sum[:, l:l + 1], scalar=lam_neg,
                                             in1=l_inv[:, r + 1:r + 2], op0=ALU.mult, op1=ALU.mult)\
                        .then_inc(c_done, 1)
                    dve.wait_ge(c_done, m + 1)
                    e2 = e2_buf[:, km % 4 * S:(km % 4 + 1) * S]
                    dve.tensor_scalar(e2, e2, mix_c[:, e:e + 1], None, ALU.mult).then_inc(scaled, 1)
                if now(g, k):
                    row_max(g, k, 1)
                if k % TB == 1 and now(g, k, -TB):
                    k_high(g * 2 + k // TB + 1, (k // TB + 1) % 2)
                if j == 1 and now(g, k - j, 2 * QB):
                    dve.wait_ge(y_mm, g * (BODY // QB) + kb - 1)
                    tile0 = (g * 2 + kb // 2 - 1) // H * TB + (kb % 2) * QB
                    for t in range(QB):
                        tile = y_acc[:, bass.ds((tile0 + t) * E, E)]
                        r1 = (((kb - 2) * QB + t) % BODY) * 2
                        add = dve.scalar_tensor_tensor(out=tile, in0=o_ps[:, t * E:(t + 1) * E],
                                                       scalar=l_inv[:, r1:r1 + 1], in1=tile,
                                                       op0=ALU.mult, op1=ALU.add)
                    add.then_inc(y_evac, 1)

            k_high(0, 0)
            attention(dve, step, QB + 2)

            dve.wait_ge(set_step, SET_STEPS)
            dve.tensor_copy(w1_hi, w1_raw[:, :]).then_inc(w1_split, 1)
            dve.wait_ge(w1_split, 1)
            dve.tensor_tensor(w1_lo, w1_raw[:, :], w1_hi.bitcast(F32), ALU.subtract).then_inc(w1_split, 1)
            dve.wait_ge(y_evac, STEPS // QB)
            dve.tensor_reduce(sum_x, y3, AX.X, ALU.add).then_inc(lny, 1)
            dve.wait_ge(lny, 1)
            dve.tensor_scalar(mean_x, sum_x, 1.0 / E, None, ALU.mult).then_inc(lny, 1)

            for u in range(UNITS + 1):
                if u < UNITS:
                    z, t = z_buf[u % 2], t_buf[u % 2]
                    dve.wait_ge(z_done, u + 1)
                    dve.tensor_scalar(t, t, GELU_A, 1.0, ALU.mult, ALU.add).then_inc(g_step, 1)
                    dve.wait_ge(g_step, 2 * u + 1)
                    dve.tensor_tensor(t, t, z, ALU.mult).then_inc(g_step, 1)
                if u >= 1:
                    z, t = z_buf[(u - 1) % 2], t_buf[(u - 1) % 2]
                    dve.wait_ge(tanh_done, u)
                    after(dve, out_mm, u - 4)
                    dve.scalar_tensor_tensor(out=hidden[(u - 1) % 4], in0=t, scalar=1.0, in1=z,
                                             op0=ALU.add, op1=ALU.mult).then_inc(h_done, 1)
                if u == UNITS // 4:
                    dve.wait_ge(lny_pool, 2)
                    dve.tensor_reduce(sum_x, y_sq, AX.X, ALU.add).then_inc(lny, 1)
                    dve.wait_ge(lny, 3)
                    dve.tensor_scalar(var_x, sum_x, 1.0 / E, LN_EPS, ALU.mult, ALU.add).then_inc(lny, 1)
                if u == UNITS // 3 + 1:
                    dve.wait_ge(lny_sqrt, 1)
                    inv_std(slice(0, NT), lny, 4)
                for b in range(B):
                    if u == min((b + 1) * UNITS // B + 3, UNITS):
                        for quad in range(2):
                            if b == 0 and quad == 0:
                                dve.wait_ge(res_ready, 1)
                            dve.wait_ge(out_mm, (b + 1) * UNITS // B)
                            i = 2 * b + quad
                            bank = ps[:, (4 + i) * BANK:(5 + i) * BANK]
                            part = y_acc[:, i * BANK:(i + 1) * BANK]
                            dve.tensor_tensor(part, part, bank, ALU.add).then_inc(f_out, 1)


_INS = ["L0_attn_X", "L0_attn_Wq", "L0_attn_bq", "L0_attn_Wk", "L0_attn_bk", "L0_attn_Wv", "L0_attn_bv",
        "L0_attn_Wo", "L0_attn_bo", "L0_attn_gamma", "L0_attn_beta", "L0_attn_lam", "L0_ffn_alpha",
        "L0_ffn_w_gate", "L0_ffn_b_gate", "L0_ffn_W1m", "L0_ffn_b1m", "L0_ffn_W2m", "L0_ffn_b2m",
        "L0_ffn_W1e", "L0_ffn_b1e", "L0_ffn_W2e", "L0_ffn_b2e"]


def kernel(**inputs):
    import numpy as np
    import concourse.bacc as bacc
    from concourse.bass_utils import run_bass_kernel_spmd

    nc = bacc.Bacc("TRN2", target_bir_lowering=False, num_devices=1)
    arrays, args = {}, []
    for name in _INS:
        a = np.asarray(inputs[name])
        if name in ("L0_attn_bq", "L0_attn_bk"):
            a = a.T
        elif name in ("L0_ffn_b1m", "L0_ffn_b1e"):
            a = np.swapaxes(a.reshape(a.shape[:-1] + (HC, P)), -1, -2)
        a = np.ascontiguousarray(a)
        arrays[f"in_{name}"] = a
        args.append(nc.dram_tensor(f"in_{name}", a.shape, mybir.dt.from_np(a.dtype), kind="ExternalInput").ap())
    args.append(nc.dram_tensor("out", (B, S, E), F32, kind="ExternalOutput").ap())
    build(nc, *args)
    r = run_bass_kernel_spmd(nc, [arrays], core_ids=[0])
    return r.results[0]["out"]
```

```python
from contextlib import ExitStack

import concourse.bass as bass
from concourse import mybir

F32 = mybir.dt.float32
F32R = mybir.dt.float32r
U32 = mybir.dt.uint32
ALU = mybir.AluOpType
ACT = mybir.ActivationFunctionType
AX = mybir.AxisListType

P = 128
B, S, E = 2, 1024, 128
H, D = 16, 64
TOK = B * S
NT = TOK // P
TB = S // P
IT = B * H
STEPS = IT * TB
QB = 4
KC = S // P
HID, NEXP, TOPK = 512, 8, 2
HC = HID // P
SETS = 1 + B * TOPK
LAG = 3
BANK = 512
UNITS = B * (1 + TOPK) * HC
SET_STEPS = 4 + 2 * SETS + 4 * B
OUT_LAG = 3
GELU_LAG = 2
Z_BUFS = 4
SQRT_AT = 10
BODY = 2 * TB
LN_EPS = 1e-5
OUT_SCALE = 0.2
QK_SCALE = 0.125
GELU_A, GELU_C = 0.044715, 0.7978845608028654


def build(nc, X, Wq, bq, Wk, bk, Wv, bv, Wo, bo, gamma, beta, lam,
          alpha, w_gate, b_gate, W1m, b1m, W2m, b2m, W1e, b1e, W2e, b2e, out):
    q_scratch = nc.dram_tensor("q_scratch", (IT, P, S), F32, kind="Internal").ap()
    k_scratch = nc.dram_tensor("k_scratch", (IT, P, S), F32, kind="Internal").ap()
    v_scratch = nc.dram_tensor("v_scratch", (IT, P, KC * D), F32, kind="Internal").ap()
    gate_scratch = nc.dram_tensor("gate_scratch", (1, B * TOPK), F32, kind="Internal").ap()

    with ExitStack() as ctx:
        def sb(name, cols, dt=F32):
            return ctx.enter_context(nc.sbuf_tensor(name, [P, cols], dt))

        def sem(name):
            return ctx.enter_context(nc.semaphore(name))

        x_all = sb("x_all", NT * E)
        x3 = x_all[:, :].rearrange("p (t e) -> p t e", e=E)
        xT_hi = sb("xT_hi", TOK, F32R)
        xT_lo = sb("xT_lo", TOK, F32R)
        y_acc = sb("y_acc", NT * E)
        y3 = y_acc[:, :].rearrange("p (t e) -> p t e", e=E)
        wo_dup = sb("wo_dup", H * E)
        wo3 = wo_dup[:, :].rearrange("p (h e) -> p h e", e=E)
        work = sb("work", 8192)
        pt = sb("pt", 8192)
        q_st = sb("q_st", 2 * 2 * S, F32R)
        k_hi = sb("k_hi", 2 * 2 * S, F32R)
        k_lo = sb("k_lo", 2 * 2 * S, F32R)
        v_h = sb("v_h", 2 * KC * D)
        p_mix = sb("p_mix", 4 * S)
        o_t = sb("o_t", 2 * BANK)
        ident = sb("ident", P)
        w1_raw = sb("w1_raw", SETS * HID)
        w2 = sb("w2", SETS * HC * E)
        bq_col = sb("bq_col", H)
        bk_col = sb("bk_col", H)
        b1_col = sb("b1_col", SETS * HC)
        b2_bc = sb("b2_bc", SETS * E)
        gb_bc = sb("gb_bc", 3 * E)
        small = sb("small", 512)
        top_idx = sb("top_idx", 8, U32)

        sum_x, mean_x, var_x = (small[:, i * NT:(i + 1) * NT] for i in range(3))
        std_x, rstd_x, tmp_x = (small[:, i * NT:(i + 1) * NT] for i in range(3, 6))
        rowsum = small[:, 96:100]
        mean_tok = small[:, 100:102]
        lam_neg = small[:, 102:103]
        a_mix = small[:, 103:104]
        a_rest = small[:, 104:105]
        coef = small[:, 105:105 + SETS]
        coef_half = small[:, 110:110 + SETS]
        gates = small[:, 116:120]
        logit, prob = small[0:B, 120:128], small[0:B, 128:136]
        lg_max, lg_sum = small[0:B, 136:137], small[0:B, 137:138]
        top8 = small[0:B, 138:146]
        gate_w = small[0:B, 146:148]
        bg_bc = small[0:B, 148:156]
        neg_max = small[:, 160:164]
        l_sum = small[:, 164:172]
        l1_neg = small[:, 172:174]
        l_inv = small[:, 176:176 + 32]
        wg = small[:, 208:216]
        lam_in = small[:, 216:217]
        al_in = small[:, 217:218]
        bq_s = small[:, 224:240]
        bq_now = small[:, 240:242]
        zero = small[:, 242:243]

        raw_q, raw_k = work[:, 0:2 * S], work[:, 2 * S:4 * S]
        e2_buf = work[:, 4 * S:8 * S]
        pt4 = pt[:, :].rearrange("p (n c q) -> p n c q", n=2, c=KC)
        qs4 = q_st[:, :].rearrange("p (n s t) -> p n s t", n=2, s=2)
        kh4 = k_hi[:, :].rearrange("p (n s t) -> p n s t", n=2, s=2)
        kl4 = k_lo[:, :].rearrange("p (n s t) -> p n s t", n=2, s=2)
        vh4 = v_h[:, :].rearrange("p (n c d) -> p n c d", n=2, c=KC)
        bv_bc = o_t[:, :]
        wqk_raw = v_h[:, KC * D:KC * D + 4 * P]
        wqk_hi, wqk_lo = k_hi[:, 2 * S:2 * S + 4 * P], k_lo[:, 2 * S:2 * S + 4 * P]
        wv_raw = w1_raw[:, 0:H * D]
        wv_hi, wv_lo = k_hi[:, 0:H * D], k_lo[:, 0:H * D]
        v_st = [t[:, :].rearrange("p (h c d) -> p h c d", h=H, c=KC) for t in (pt, work)]
        qk_out = pt[:, :].rearrange("p (n w t) -> p n w t", n=2, w=2)
        w1_hi, w1_lo = ([t[:, i * HID:(i + 1) * HID] for i in range(SETS - 1)] for t in (q_st, k_hi))
        w1_hi.append(k_lo[:, 0:HID])
        w1_lo.append(k_lo[:, HID:2 * HID])
        hidden = [pt[:, i * S:(i + 1) * S] for i in range(4)]
        z_buf = [work[:, i * S:(i + 1) * S] for i in range(Z_BUFS)]
        t_buf = [work[:, (4 + i) * S:(5 + i) * S] for i in range(Z_BUFS)]
        y_sq = pt[:, 4 * S:6 * S].rearrange("p (t e) -> p t e", e=E)
        w1r3 = w1_raw[:, :].rearrange("p (s n) -> p s n", s=SETS)
        w24 = w2[:, :].rearrange("p (s c e) -> p s c e", s=SETS, c=HC)

        ps = ctx.enter_context(nc.psum_tensor("ps", [P, 8 * BANK], F32))
        slot = [ps[:, i * S:(i + 1) * S] for i in range(3)]
        pt_ps = ps[:, 6 * BANK:7 * BANK]
        o_ps = ps[:, 7 * BANK:8 * BANK]

        x_loaded = [sem(f"x_loaded{b}") for b in range(B)]
        small_loaded, bias_loaded = sem("small_loaded"), sem("bias_loaded")
        wv_loaded, wo_loaded, experts_loaded = sem("wv_loaded"), sem("wo_loaded"), sem("experts_loaded")
        id_ready, ln_step, sqrt_done = sem("id_ready"), sem("ln_step"), sem("sqrt_done")
        xn_ready, xt_ps, xt_hi, xt_lo = sem("xn_ready"), sem("xt_ps"), sem("xt_hi"), sem("xt_lo")
        wv_split, v_mm, v_evac = sem("wv_split"), sem("v_mm"), sem("v_evac")
        v_stored = [sem(f"v_stored{b}") for b in range(B)]
        route, route_mm, route_act = sem("route"), sem("route_mm"), sem("route_act")
        gates_out, gates_in, set_step = sem("gates_out"), sem("gates_in"), sem("set_step")
        bqs_ready, bq_col_ready = sem("bqs_ready"), sem("bq_col_ready")
        w_loaded = [sem(f"w_loaded{i}") for i in range(2)]
        w_split, q_mm, k_mm, q_evac, k_evac = (sem("w_split"), sem("q_mm"), sem("k_mm"), sem("q_evac"),
                                               sem("k_evac"))
        qk_stored = [sem(f"qk_stored{i}") for i in range(2)]
        raw_loaded = sem("raw_loaded")
        v_loaded = [sem(f"v_loaded{i}") for i in range(2)]
        khi_done, qhi_done, split_done = sem("khi_done"), sem("qhi_done"), sem("split_done")
        s_ready, max_done, exp_done = sem("s_ready"), sem("max_done"), sem("exp_done")
        recip_done = sem("recip_done")
        scaled, mix_done = sem("scaled"), sem("mix_done")
        pt_ready, pt_evac = sem("pt_ready"), sem("pt_evac")
        pv_done, o_evac, y_mm, y_evac = sem("pv_done"), sem("o_evac"), sem("y_mm"), sem("y_evac")
        w1_split, h_mm, z_done = sem("w1_split"), sem("h_mm"), sem("z_done")
        cubic, arg_done = sem("cubic"), sem("arg_done")
        tanh_done, h_done, out_mm, f_out = sem("tanh_done"), sem("h_done"), sem("out_mm"), sem("f_out")
        lny, lny_sqrt = sem("lny"), sem("lny_sqrt")
        stored = sem("stored")

        def after(eng, s, count):
            if not isinstance(count, int) or count > 0:
                eng.wait_ge(s, count)

        def now(g, k, lag=0):
            return not isinstance(g, int) or 0 <= g * BODY + k - lag < STEPS

        def attention(eng, step, lag, beside=None):
            for k in range(BODY):
                step(0, k)
            with eng.Fori(1, STEPS // BODY - 1) as g:
                for k in range(BODY):
                    step(g, k)
            for k in range(BODY):
                step(STEPS // BODY - 1, k)
            for k in range(lag):
                step(STEPS // BODY, k)
                if beside:
                    beside(k)

        SLOT = [k % 3 for k in range(2 * BODY)]

        def last_user(k):
            return next(d for d in range(1, 2 * BODY + 1) if SLOT[(k - d) % (2 * BODY)] == SLOT[k])

        block = ctx.enter_context(nc.Block())

        @block.sync
        def _(sp):
            xv = X.rearrange("b (t p) e -> p (b t) e", p=P)
            for b in range(B):
                sp.dma_start(x3[:, b * TB:(b + 1) * TB, :], xv[:, b * TB:(b + 1) * TB, :]).then_inc(x_loaded[b], 16)
            sp.dma_start(wv_raw.rearrange("p (h d) -> p h d", h=H), Wv.rearrange("h e d -> e h d"))\
                .then_inc(wv_loaded, 16)
            sp.dma_start(bv_bc, bv.rearrange("h d -> (h d)").partition_broadcast(P)).then_inc(bias_loaded, 16)
            for i, v in enumerate((gamma, beta, bo)):
                sp.dma_start(gb_bc[:, i * E:(i + 1) * E], v.partition_broadcast(P)).then_inc(bias_loaded, 16)
            for half in range(2):
                sp.dma_start(wo3[half * D:(half + 1) * D, :, :], Wo.rearrange("(h d) e -> d h e", d=D))\
                    .then_inc(wo_loaded, 16)

            def load_set(s_, w1, b1, w2_, b2):
                sp.dma_start(w1r3[:, s_, :], w1).then_inc(experts_loaded, 16)
                sp.dma_start(w24[:, s_, :, :], w2_.rearrange("(c p) e -> p c e", p=P)).then_inc(experts_loaded, 16)
                sp.dma_start(b1_col[:, s_ * HC:(s_ + 1) * HC], b1).then_inc(experts_loaded, 16)
                sp.dma_start(b2_bc[:, s_ * E:(s_ + 1) * E], b2.partition_broadcast(P)).then_inc(experts_loaded, 16)

            sp.wait_ge(wv_split, 2)
            load_set(0, W1m, b1m, W2m, b2m)

            for b in range(B):
                sp.wait_ge(v_evac, 2 * TB * (b + 1))
                sp.dma_start(v_scratch[b * H:(b + 1) * H, :, :].rearrange("h p n -> p h n"),
                             (pt, work)[b][:, :].rearrange("p (h n) -> p h n", h=H)).then_inc(v_stored[b], 16)

            sp.wait_ge(route, 14)
            sp.dma_start(gate_scratch.rearrange("o (b k) -> (o b) k", b=B), gate_w).then_inc(gates_out, 16)
            for b in range(B):
                for c in range(TOPK):
                    e = sp.value_load(top_idx[b:b + 1, c:c + 1], min_val=0, max_val=NEXP - 1)
                    load_set(1 + TOPK * b + c, W1e[bass.ds(e, 1), :, :].rearrange("o a n -> (o a) n"),
                             b1e[bass.ds(e, 1), :, :].rearrange("o p c -> (o p) c"),
                             W2e[bass.ds(e, 1), :, :].rearrange("o n e -> (o n) e"),
                             b2e[bass.ds(e, 1), :].rearrange("o n -> (o n)"))
            sp.wait_ge(gates_out, 16)
            sp.dma_start(gates, gate_scratch.rearrange("o n -> (o n)").partition_broadcast(P))\
                .then_inc(gates_in, 16)

            def store_qk(g, par):
                h = 2 * g + par
                sp.wait_ge(q_evac, 2 * h + 2)
                sp.dma_start(q_scratch.rearrange("(b h) p t -> h p b t", b=B)[bass.ds(h, 1), :, :, :]
                             .rearrange("o p b t -> (o p) b t"),
                             qk_out[:, par, 0, :].rearrange("p (b t) -> p b t", b=B)).then_inc(qk_stored[par], 16)
                sp.wait_ge(k_evac, 2 * h + 2)
                sp.dma_start(k_scratch.rearrange("(b h) p t -> h p b t", b=B)[bass.ds(h, 1), :, :, :]
                             .rearrange("o p b t -> (o p) b t"),
                             qk_out[:, par, 1, :].rearrange("p (b t) -> p b t", b=B)).then_inc(qk_stored[par], 16)

            def load(i, par):
                after(sp, split_done, 8 * i)
                for half in range(2):
                    rows = slice(half * D, (half + 1) * D)
                    for dst, src in ((raw_q, q_scratch), (raw_k, k_scratch)):
                        sp.dma_start(dst[rows, :].rearrange("p (s t) -> p s t", s=2),
                                     src[bass.ds(i, 1), :, :].rearrange("o (s d) t -> (o d) s t", d=D))\
                            .then_inc(raw_loaded, 16)
                after(sp, pv_done, 2 * i - 2)
                sp.dma_start(v_h[:, par * KC * D:(par + 1) * KC * D],
                             v_scratch[bass.ds(i, 1), :, :].rearrange("o p n -> (o p) n"))\
                    .then_inc(v_loaded[par], 16)

            with sp.Fori(0, 2) as g:
                for par in range(2):
                    store_qk(g, par)
            sp.wait_ge(qk_stored[0], 32)
            for b in range(B):
                sp.wait_ge(v_stored[b], 16)
            load(0, 0)
            with sp.Fori(2, H // 2) as g:
                for par in range(2):
                    store_qk(g, par)
            for par in range(2):
                sp.wait_ge(qk_stored[par], 32 * (H // 2))
            load(1, 1)
            with sp.Fori(1, IT // 2) as g:
                for par in range(2):
                    load(2 * g + par, par)

            ov = out.rearrange("b (t p) e -> p (b t) e", p=P)
            for i in range(NT // 4):
                sp.wait_ge(f_out, i + 1)
                sp.dma_start(ov[:, 4 * i:4 * i + 4, :], y3[:, 4 * i:4 * i + 4, :]).then_inc(stored, 16)
            sp.wait_ge(stored, 16 * NT // 4)

        @block.gpsimd
        def _(pool):
            pool.memset(ident[:, :], 0.0).then_inc(id_ready, 1)
            pool.wait_ge(id_ready, 1)
            pool.affine_select(out=ident[:, :], in_=ident[:, :], compare_op=ALU.not_equal, fill=1.0,
                               base=0, pattern=[[-1, P]], channel_multiplier=1).then_inc(id_ready, 1)
            pool.dma_start(wg, w_gate).then_inc(small_loaded, 16)
            pool.dma_start(bg_bc, b_gate.partition_broadcast(B)).then_inc(small_loaded, 16)
            pool.dma_start(lam_in, lam.partition_broadcast(P)).then_inc(small_loaded, 16)
            pool.dma_start(al_in, alpha.partition_broadcast(P)).then_inc(small_loaded, 16)

            pool.memset(zero, 0.0).then_inc(id_ready, 1)

            pool.wait_ge(wv_loaded, 16)
            pool.tensor_copy(wv_hi, wv_raw).then_inc(wv_split, 1)
            pool.wait_ge(wv_split, 1)
            pool.tensor_tensor(wv_lo, wv_raw, wv_hi.bitcast(F32), ALU.subtract).then_inc(wv_split, 1)

            def split_w(g, par, first):
                h = 2 * g + par
                sl = slice(par * 2 * P, (par + 1) * 2 * P)
                pool.wait_ge(w_loaded[par], 32 * g + 32)
                if not first:
                    pool.wait_ge(k_mm, 2 * h - 2)
                pool.tensor_tensor(wqk_hi[:, sl], wqk_raw[:, sl], zero.to_broadcast([P, 2 * P]), ALU.subtract)\
                    .then_inc(w_split, 1)
                pool.wait_ge(w_split, 2 * h + 1)
                pool.tensor_tensor(wqk_lo[:, sl], wqk_raw[:, sl], wqk_hi[:, sl].bitcast(F32), ALU.subtract)\
                    .then_inc(w_split, 1)

            pool.wait_ge(id_ready, 3)
            for par in range(2):
                split_w(0, par, True)
            def split_k(i, par, quarter):
                a = quarter * BANK
                c0 = par * 2 * S + a
                pool.wait_ge(khi_done, i + 1)
                pool.tensor_tensor(k_lo[:, bass.ds(c0, BANK)], raw_k[:, bass.ds(a, BANK)],
                                   k_hi[:, bass.ds(c0, BANK)].bitcast(F32), ALU.subtract).then_inc(split_done, 1)

            def split_q(i, par, quarter, own, count, done):
                a = quarter * BANK
                low = q_st[D:P, bass.ds(par * 2 * S + a, BANK)]
                pool.wait_ge(own, count)
                pool.wait_ge(split_done, done - 1)
                pool.wait_ge(qhi_done, i + 1)
                pool.tensor_tensor(low, raw_q[D:P, bass.ds(a, BANK)], low.bitcast(F32), ALU.subtract)\
                    .then_inc(split_done, 1)
                pool.wait_ge(split_done, done)

            with pool.Fori(1, H // 4) as g:
                for par in range(2):
                    split_w(g, par, False)
            with pool.Fori(H // 4, H // 2) as g:
                quarter = g - H // 4
                split_w(g, 0, False)
                split_k(0, 0, quarter)
                split_w(g, 1, False)
                split_q(0, 0, quarter, w_split, 4 * g + 4, 2 * quarter + 2)

            def step(g, k):
                n = g * BODY + k
                if now(g, k, 1):
                    e1 = p_mix[:, (k - 1) % 4 * S:((k - 1) % 4 + 1) * S]
                    e2 = e2_buf[:, (k - 1) % 4 * S:((k - 1) % 4 + 1) * S]
                    pool.wait_ge(scaled, n)
                    pool.tensor_tensor(e1, e1, e2, ALU.add).then_inc(mix_done, 1)
                if k % TB in SPLIT_AT and now(g, k, -TB):
                    i, par = g * 2 + k // TB + 1, (k // TB + 1) % 2
                    for part in SPLIT_AT[k % TB]:
                        if part < 4:
                            split_k(i, par, part)
                        else:
                            split_q(i, par, part - 4, mix_done, n, 8 * i + part + 1)
                s_ = k - TB - 1
                if isinstance(g, int) and g == STEPS // BODY - 1 and 0 <= s_ < SETS:
                    pool.wait_ge(s_ready, 2 * TB * (IT - 1))
                    pool.tensor_tensor(w1_hi[s_], w1r3[:, s_, :], zero.to_broadcast([P, HID]), ALU.subtract)\
                        .then_inc(w1_split, 1)
                    pool.wait_ge(w1_split, 2 * s_ + 1)
                    pool.tensor_tensor(w1_lo[s_], w1r3[:, s_, :], w1_hi[s_].bitcast(F32), ALU.subtract)\
                        .then_inc(w1_split, 1)

            SPLIT_AT = {1: (0, 1), 2: (2,), 3: (3,), 4: (4, 5), 5: (6,), 6: (7,)}
            attention(pool, step, 1)

            for u in range(UNITS):
                z, t = z_buf[u % Z_BUFS], t_buf[u % Z_BUFS]
                pool.wait_ge(cubic, u + 1)
                pool.tensor_tensor(t, t, z, ALU.mult).then_inc(arg_done, 1)

        @block.tensor
        def _(pe):
            pe.wait_ge(id_ready, 2)
            for i in range(NT):
                if i % 8 == 0:
                    pe.wait_ge(xn_ready, i // 8 + 1)
                mm = pe.transpose(ps[:, i * P:(i + 1) * P], p_mix[:, i * E:(i + 1) * E], ident[:, :])
                if i % 4 == 3:
                    mm.then_inc(xt_ps, 1)
            pe.wait_ge(wv_split, 2)
            for i in range(NT):
                for hv in range(2):
                    u = 2 * i + hv
                    bank = 4 + u % 4
                    if u % 8 == 0:
                        pe.wait_ge(xt_lo, i // 4 + 1)
                    after(pe, v_evac, u - 3)
                    for j, (a, w) in enumerate(((xT_hi, wv_hi), (xT_lo, wv_hi), (xT_hi, wv_lo))):
                        mm = pe.matmul(ps[:, bank * BANK:(bank + 1) * BANK], a[:, i * P:(i + 1) * P],
                                       w[:, hv * BANK:(hv + 1) * BANK], start=j == 0, stop=j == 2)
                    mm.then_inc(v_mm, 1)
            pe.wait_ge(route, 2)
            pe.wait_ge(small_loaded, 64)
            pe.matmul(ps[0:B, 0:NEXP], mean_tok, wg, start=True, stop=True).then_inc(route_mm, 1)

            pe.wait_ge(v_evac, 2 * NT)
            pe.wait_ge(route, 3)

            def project(g, par, first):
                h = 2 * g + par
                pe.wait_ge(w_split, 2 * h + 2)
                for w, evac, mm_sem in ((0, q_evac, q_mm), (1, k_evac, k_mm)):
                    for half in range(2):
                        if not first:
                            pe.wait_ge(evac, 2 * h - 1 + half)
                        for j, (wt, a) in enumerate(((wqk_hi, xT_hi), (wqk_lo, xT_hi), (wqk_hi, xT_lo))):
                            c0 = (par * 2 + w) * P
                            for q in range(2):
                                col = half * S + q * BANK
                                mm = pe.matmul(ps[:, w * 2 * S + col:w * 2 * S + col + BANK],
                                               wt[:, c0:c0 + P], a[:, col:col + BANK], start=j == 0, stop=j == 2)
                        mm.then_inc(mm_sem, 1)

            project(0, 0, True)
            project(0, 1, False)
            with pe.Fori(1, H // 2) as g:
                for par in range(2):
                    project(g, par, False)

            pe.wait_ge(q_evac, 2 * H)
            pe.wait_ge(k_evac, 2 * H)

            def scores(g, k, s):
                tile = 2 * k + s
                n = g * BODY + k
                after(pe, exp_done, 2 * n + s + 1 - last_user(tile))
                par, q0 = k // TB, (k % TB) * P
                for j, kk in enumerate((kh4, kl4)):
                    for half in range(2):
                        cols = slice(half * BANK, (half + 1) * BANK)
                        mm = pe.matmul(slot[SLOT[tile]][:, cols], qs4[:, par, s, q0:q0 + P], kk[:, par, s, cols],
                                       start=j == 0, stop=j == 1)
                mm.then_inc(s_ready, 1)

            def turn(g, k, half):
                n = g * BODY + k - LAG
                if half == 0:
                    pe.wait_ge(mix_done, n + 1)
                after(pe, pt_evac, 2 * n + half)
                for c in range(4):
                    col = (k - LAG) % 4 * S + (half * 4 + c) * P
                    mm = pe.transpose(pt_ps[:, c * P:(c + 1) * P], p_mix[:, col:col + P], ident[:, :])
                mm.then_inc(pt_ready, 1)

            def pv(g, kb, c0):
                blk = g * (BODY // QB) + kb
                if c0 == 0:
                    pe.wait_ge(pt_evac, 2 * QB * (blk + 1))
                    after(pe, y_evac, blk)
                    if kb % 2 == 0:
                        pe.wait_ge(v_loaded[kb // 2], 16 * (g + 1))
                for c in (c0, c0 + 1):
                    half = c % 2
                    mm = pe.matmul(o_ps[half * D:(half + 1) * D, :], vh4[:, (kb // 2) % 2, c, :],
                                   pt4[:, kb % 2, c, :], start=c < 2, stop=c >= KC - 2,
                                   skip_group_check=True)
                if c0 == KC - 2:
                    mm.then_inc(pv_done, 1)

            def out_proj(g, kb):
                head = (g * 2 + kb // 2 - 1) % H
                pe.wait_ge(o_evac, g * (BODY // QB) + kb - 1)
                for t in range(QB):
                    col = (kb % 2) * BANK + t * P
                    mm = pe.matmul(o_ps[:, t * E:(t + 1) * E], o_t[:, col:col + P],
                                   wo_dup[:, bass.ds(head * E, E)], start=True, stop=True, skip_group_check=True)
                mm.then_inc(y_mm, 1)

            def step(g, k):
                kb, j = divmod(k, QB)
                if now(g, k):
                    if k % TB == 0:
                        pe.wait_ge(split_done, 8 * (g * 2 + k // TB) + 8)
                    scores(g, k, 0)
                if now(g, k, LAG):
                    turn(g, k, 0)
                if j == 1 and now(g, k - j, 2 * QB):
                    out_proj(g, kb)
                if j == 3 and now(g, k - j, QB):
                    pv(g, kb - 1, 0)
                if j == 0 and now(g, k, 2 * QB):
                    pv(g, kb - 2, 4)
                if now(g, k):
                    scores(g, k, 1)
                if now(g, k, LAG):
                    turn(g, k, 1)
                if j == 3 and now(g, k - j, QB):
                    pv(g, kb - 1, 2)
                if j == 0 and now(g, k, 2 * QB):
                    pv(g, kb - 2, 6)


            def hidden_mm(u):
                b, i = divmod(u, (1 + TOPK) * HC)
                f, c = divmod(i, HC)
                set_ = 0 if f == 0 else TOPK * b + f
                after(pe, z_done, u - 2)
                for j, (w, a) in enumerate(((w1_hi, xT_hi), (w1_lo, xT_hi), (w1_hi, xT_lo))):
                    for half in range(2):
                        t0 = b * S + half * BANK
                        mm = pe.matmul(slot[u % 3][:, half * BANK:(half + 1) * BANK],
                                       w[set_][:, c * P:(c + 1) * P],
                                       a[:, t0:t0 + BANK], start=j == 0, stop=j == 2)
                mm.then_inc(h_mm, 1)

            def output_mm(u):
                b, i = divmod(u, (1 + TOPK) * HC)
                f, c = divmod(i, HC)
                pe.wait_ge(h_done, u + 1)
                if i == 0:
                    after(pe, f_out, 2 * b)
                for t in range(TB):
                    out_ps = ps[:, 6 * BANK + t * E:6 * BANK + (t + 1) * E]
                    mm = pe.matmul(out_ps, hidden[u % 4][:, t * P:(t + 1) * P],
                                   w24[:, 0 if f == 0 else TOPK * b + f, c, :],
                                   start=i == 0 and t % 4 == 0, stop=i == (1 + TOPK) * HC - 1,
                                   skip_group_check=True)
                mm.then_inc(out_mm, 1)

            def start_hidden(k):
                if k == 1:
                    pe.wait_ge(exp_done, 2 * STEPS)
                    pe.wait_ge(w1_split, 2 * SETS)
                if 1 <= k <= OUT_LAG:
                    hidden_mm(k - 1)

            pe.wait_ge(wo_loaded, 32)
            attention(pe, step, QB + 2, start_hidden)

            for u in range(OUT_LAG, UNITS + OUT_LAG):
                if u < UNITS:
                    hidden_mm(u)
                if u == OUT_LAG:
                    pe.wait_ge(y_evac, STEPS // QB)
                    pe.wait_ge(set_step, SET_STEPS)
                if u >= OUT_LAG:
                    output_mm(u - OUT_LAG)

        @block.scalar
        def _(act):
            act.dma_start(bq_col[:, :], bq).then_inc(bias_loaded, 16)
            act.dma_start(bk_col[:, :], bk).then_inc(bias_loaded, 16)

            def load_w(g, par):
                h = 2 * g + par
                for w, src in enumerate((Wq, Wk)):
                    c0 = (par * 2 + w) * P
                    act.dma_start(wqk_raw[:, c0:c0 + P],
                                  src[bass.ds(h, 1), :, :].rearrange("o e c -> (o e) c")).then_inc(w_loaded[par], 16)

            load_w(0, 0)
            load_w(0, 1)
            for b in range(B):
                act.wait_ge(ln_step, 10 * b + 6)
                act.activation(std_x[:, b * TB:(b + 1) * TB], var_x[:, b * TB:(b + 1) * TB], ACT.Sqrt)\
                    .then_inc(sqrt_done, 1)
            for i in range(NT // 4):
                act.wait_ge(xt_ps, i + 1)
                act.activation(xT_hi[:, i * BANK:(i + 1) * BANK], ps[:, i * BANK:(i + 1) * BANK], ACT.Copy,
                               accum_out=rowsum[:, i:i + 1]).then_inc(xt_hi, 1)
            act.wait_ge(bias_loaded, 96)
            act.mul(bq_s, bq_col[:, :], QK_SCALE).then_inc(bqs_ready, 1)
            act.wait_ge(bqs_ready, 1)
            act.wait_ge(route, 5)
            act.activation(prob, logit, ACT.Exp, bias=lg_max, scale=1.0, accum_out=lg_sum).then_inc(route_act, 1)

            act.wait_ge(v_stored[0], 16)

            def evac_q(g, par, first):
                h = 2 * g + par
                act.activation(bq_now[:, par:par + 1], bq_s[:, bass.ds(h, 1)], ACT.Copy).then_inc(bq_col_ready, 1)
                if not first:
                    act.wait_ge(qk_stored[par], 32 * g)
                act.wait_ge(bq_col_ready, h + 1)
                for half in range(2):
                    act.wait_ge(q_mm, 2 * h + half + 1)
                    act.activation(qk_out[:, par, 0, half * S:(half + 1) * S], ps[:, half * S:(half + 1) * S],
                                   ACT.Identity, bias=bq_now[:, par:par + 1], scale=QK_SCALE).then_inc(q_evac, 1)

            def next_w(g, par):
                act.wait_ge(w_split, 2 * (2 * g + par) + 2)
                load_w(g + 1, par)

            for par in range(2):
                next_w(0, par)
                evac_q(0, par, True)
            def q_high(i, par):
                act.wait_ge(raw_loaded, 64 * (i + 1))
                after(act, s_ready, 2 * TB * (i - 1))
                act.activation(q_st[:, par * 2 * S:(par + 1) * 2 * S], raw_q, ACT.Copy).then_inc(qhi_done, 1)

            with act.Fori(1, H // 4) as g:
                for par in range(2):
                    next_w(g, par)
                    evac_q(g, par, False)
            q_high(0, 0)
            with act.Fori(H // 4, H // 2 - 1) as g:
                for par in range(2):
                    next_w(g, par)
                    evac_q(g, par, False)
            for par in range(2):
                evac_q(H // 2 - 1, par, False)

            act.wait_ge(v_stored[1], 16)

            def exps(g, k, s):
                n = g * BODY + k
                act.wait_ge(max_done, 2 * n + s + 1)
                if s == 0:
                    after(act, pt_ready, 2 * (n - 3))
                else:
                    after(act, mix_done, n - 3)
                m, l = (k % 2) * 2 + s, (k % 4) * 2 + s
                act.activation((p_mix, e2_buf)[s][:, k % 4 * S:(k % 4 + 1) * S], slot[SLOT[2 * k + s]], ACT.Exp,
                               bias=neg_max[:, m:m + 1], scale=1.0, accum_out=l_sum[:, l:l + 1])\
                    .then_inc(exp_done, 1)

            def evac_pt(g, k, half):
                kb, j = divmod(k - LAG, QB)
                if half == 0 and isinstance(g, int) and g * BODY + k == LAG:
                    for par in range(2):
                        act.wait_ge(qk_stored[par], 32 * (H // 2))
                if half == 0 and j == 0:
                    after(act, pv_done, g * (BODY // QB) + kb - 1)
                act.wait_ge(pt_ready, 2 * (g * BODY + k - LAG) + half + 1)
                act.activation(pt4[:, kb % 2, half * 4:half * 4 + 4, j * P:(j + 1) * P],
                               pt_ps.rearrange("p (c q) -> p c q", c=4), ACT.Copy).then_inc(pt_evac, 1)

            def step(g, k):
                kb, j = divmod(k, QB)
                if j == 1 and now(g, k - j, 2 * QB):
                    act.wait_ge(pv_done, g * (BODY // QB) + kb - 1)
                    act.activation(o_t[:, (kb % 2) * BANK:(kb % 2 + 1) * BANK], o_ps, ACT.Copy).then_inc(o_evac, 1)
                if now(g, k, LAG):
                    evac_pt(g, k, 0)
                if now(g, k):
                    exps(g, k, 0)
                if now(g, k, LAG):
                    evac_pt(g, k, 1)
                if now(g, k):
                    exps(g, k, 1)
                if k % TB == 1 and now(g, k, -TB):
                    q_high(g * 2 + k // TB + 1, (k // TB + 1) % 2)

            def gelu(u):
                if u == SQRT_AT:
                    act.wait_ge(lny, 10)
                    act.activation(std_x, var_x, ACT.Sqrt).then_inc(lny_sqrt, 1)
                if u < UNITS:
                    b, i = divmod(u, (1 + TOPK) * HC)
                    f, c = divmod(i, HC)
                    col = (0 if f == 0 else TOPK * b + f) * HC + c
                    z, t = z_buf[u % Z_BUFS], t_buf[u % Z_BUFS]
                    act.wait_ge(h_mm, u + 1)
                    if u < Z_BUFS:
                        act.wait_ge(mix_done, STEPS - Z_BUFS + u + 1)
                    after(act, h_done, u - Z_BUFS + 1)
                    act.activation(z, slot[u % 3], ACT.Identity, bias=b1_col[:, col:col + 1], scale=1.0)
                    act.activation(t, slot[u % 3], ACT.Square, bias=b1_col[:, col:col + 1], scale=1.0)\
                        .then_inc(z_done, 1)
                if u >= GELU_LAG:
                    t = t_buf[(u - GELU_LAG) % Z_BUFS]
                    act.wait_ge(arg_done, u - GELU_LAG + 1)
                    act.activation(t, t, ACT.Tanh, scale=GELU_C).then_inc(tanh_done, 1)

            def start_gelu(k):
                if k == 2:
                    act.wait_ge(set_step, SET_STEPS)
                if 2 <= k <= 4:
                    gelu(k - 2)

            attention(act, step, QB + 2, start_gelu)
            for u in range(3, UNITS + GELU_LAG):
                gelu(u)

        @block.vector
        def _(dve):
            xn3 = p_mix[:, 0:2 * S].rearrange("p (t e) -> p t e", e=E)
            sq3 = work[:, 0:S].rearrange("p (t e) -> p t e", e=E)

            def inv_std(t, s, base):
                dve.reciprocal(rstd_x[:, t], std_x[:, t]).then_inc(s, 1)
                dve.wait_ge(s, base + 1)
                dve.tensor_tensor(tmp_x[:, t], rstd_x[:, t], rstd_x[:, t], ALU.mult).then_inc(s, 1)
                dve.wait_ge(s, base + 2)
                dve.scalar_tensor_tensor(out=tmp_x[:, t], in0=tmp_x[:, t], scalar=-0.5, in1=var_x[:, t],
                                         op0=ALU.mult, op1=ALU.mult).then_inc(s, 1)
                dve.wait_ge(s, base + 3)
                dve.scalar_tensor_tensor(out=rstd_x[:, t], in0=tmp_x[:, t], scalar=1.5, in1=rstd_x[:, t],
                                         op0=ALU.add, op1=ALU.mult).then_inc(s, 1)

            for b in range(B):
                t = slice(b * TB, (b + 1) * TB)
                o = 10 * b
                dve.wait_ge(x_loaded[b], 16)
                dve.tensor_reduce(sum_x[:, t], x3[:, t, :], AX.X, ALU.add).then_inc(ln_step, 1)
                dve.wait_ge(ln_step, o + 1)
                dve.tensor_scalar(mean_x[:, t], sum_x[:, t], 1.0 / E, None, ALU.mult).then_inc(ln_step, 1)
                dve.wait_ge(ln_step, o + 2)
                dve.tensor_tensor(xn3[:, t, :], x3[:, t, :],
                                  mean_x[:, t].unsqueeze(2).to_broadcast([P, TB, E]), ALU.subtract)\
                    .then_inc(ln_step, 1)
                dve.wait_ge(ln_step, o + 3)
                dve.tensor_tensor(sq3, xn3[:, t, :], xn3[:, t, :], ALU.mult).then_inc(ln_step, 1)
                dve.wait_ge(ln_step, o + 4)
                dve.tensor_reduce(sum_x[:, t], sq3, AX.X, ALU.add).then_inc(ln_step, 1)
                dve.wait_ge(ln_step, o + 5)
                dve.tensor_scalar(var_x[:, t], sum_x[:, t], 1.0 / E, LN_EPS, ALU.mult, ALU.add)\
                    .then_inc(ln_step, 1)
                dve.wait_ge(sqrt_done, b + 1)
                inv_std(t, ln_step, o + 6)
                dve.wait_ge(ln_step, o + 10)
                dve.tensor_tensor(xn3[:, t, :], xn3[:, t, :],
                                  rstd_x[:, t].unsqueeze(2).to_broadcast([P, TB, E]), ALU.mult)\
                    .then_inc(xn_ready, 1)
            for i in range(NT // 4):
                dve.wait_ge(xt_hi, i + 1)
                dve.tensor_tensor(xT_lo[:, i * BANK:(i + 1) * BANK], ps[:, i * BANK:(i + 1) * BANK],
                                  xT_hi[:, i * BANK:(i + 1) * BANK].bitcast(F32), ALU.subtract).then_inc(xt_lo, 1)
            dve.tensor_tensor(mean_tok, rowsum[:, 0:4:2], rowsum[:, 1:4:2], ALU.add).then_inc(route, 1)
            dve.wait_ge(route, 1)
            dve.tensor_scalar(mean_tok, mean_tok, 1.0 / S, None, ALU.mult).then_inc(route, 1)

            dve.wait_ge(bias_loaded, 96)
            bv3 = bv_bc.rearrange("p (h d) -> p h d", d=D)
            for u in range(2 * NT):
                i, hv = divmod(u, 2)
                bank = 4 + u % 4
                dve.wait_ge(v_mm, u + 1)
                dve.tensor_tensor(v_st[i // TB][:, hv * 8:(hv + 1) * 8, i % TB, :],
                                  ps[:, bank * BANK:(bank + 1) * BANK].rearrange("p (h d) -> p h d", d=D),
                                  bv3[:, hv * 8:(hv + 1) * 8, :], ALU.add).then_inc(v_evac, 1)

            dve.wait_ge(route_mm, 1)
            dve.tensor_tensor(logit, ps[0:B, 0:NEXP], bg_bc, ALU.add).then_inc(route, 1)
            dve.wait_ge(route, 3)
            dve.tensor_reduce(lg_max, logit, AX.X, ALU.max, negate=True).then_inc(route, 1)
            dve.tensor_scalar(a_mix, al_in, 0.1, 1.0, ALU.max, ALU.min).then_inc(route, 1)
            dve.wait_ge(route_act, 1)
            dve.reciprocal(lg_sum, lg_sum).then_inc(route, 1)
            dve.wait_ge(route, 6)
            dve.tensor_scalar(prob, prob, lg_sum, None, ALU.mult).then_inc(route, 1)
            dve.wait_ge(route, 7)
            dve.max(top8, prob).then_inc(route, 1)
            dve.wait_ge(route, 8)
            dve.max_index(top_idx[0:B, :], top8, prob).then_inc(route, 1)
            dve.tensor_tensor(lg_sum, top8[:, 0:1], top8[:, 1:2], ALU.add).then_inc(route, 1)
            dve.wait_ge(route, 10)
            dve.reciprocal(lg_sum, lg_sum).then_inc(route, 1)
            dve.wait_ge(route, 11)
            dve.tensor_scalar(gate_w, top8[:, 0:TOPK], lg_sum, None, ALU.mult).then_inc(route, 1)
            dve.tensor_scalar(lam_neg, lam_in, -1.0, None, ALU.mult).then_inc(route, 1)
            dve.tensor_scalar(a_rest, a_mix, -1.0, 1.0, ALU.mult, ALU.add).then_inc(route, 1)

            dve.wait_ge(v_stored[0], 16)

            def evac_k(g, par, first):
                h = 2 * g + par
                if not first:
                    dve.wait_ge(qk_stored[par], 32 * g)
                for half in range(2):
                    dve.wait_ge(k_mm, 2 * h + half + 1)
                    dve.tensor_scalar(qk_out[:, par, 1, half * S:(half + 1) * S],
                                      ps[:, 2 * S + half * S:2 * S + (half + 1) * S],
                                      bk_col[:, bass.ds(h, 1)], None, ALU.add).then_inc(k_evac, 1)

            for par in range(2):
                evac_k(0, par, True)

            def evac_heads(first, end):
                with dve.Fori(first, end) as g:
                    for par in range(2):
                        evac_k(g, par, False)

            def k_high(i, par):
                dve.wait_ge(raw_loaded, 64 * (i + 1))
                after(dve, s_ready, 2 * TB * (i - 1))
                dve.tensor_copy(k_hi[:, par * 2 * S:(par + 1) * 2 * S], raw_k).then_inc(khi_done, 1)

            bias = b2_bc[:, :].rearrange("p (s e) -> p s e", s=SETS)

            def weights():
                dve.wait_ge(gates_in, 16)
                dve.tensor_scalar(coef[:, 1:SETS], gates, a_rest, None, ALU.mult).then_inc(set_step, 1)
                dve.tensor_copy(coef[:, 0:1], a_mix).then_inc(set_step, 1)
                dve.wait_ge(set_step, 2)
                dve.tensor_scalar(coef_half, coef, 0.5, None, ALU.mult).then_inc(set_step, 1)
                dve.tensor_scalar(gb_bc[:, 0:2 * E], gb_bc[:, 0:2 * E], OUT_SCALE, None, ALU.mult)\
                    .then_inc(set_step, 1)
                dve.wait_ge(experts_loaded, 64 * SETS)
                for s_ in range(SETS):
                    dve.tensor_scalar(bias[:, s_, :], bias[:, s_, :], coef[:, s_:s_ + 1], None, ALU.mult)\
                        .then_inc(set_step, 1)

            def added():
                done = 4 + SETS
                dve.wait_ge(set_step, done)
                for b in range(B):
                    first = bias[:, 1 + TOPK * b, :]
                    for v in (bias[:, 2 + TOPK * b, :], bias[:, 0, :], gb_bc[:, E:2 * E]):
                        dve.tensor_tensor(first, first, v, ALU.add).then_inc(set_step, 1)
                        done += 1
                        dve.wait_ge(set_step, done)
                    xb = x3[:, b * TB:(b + 1) * TB, :]
                    dve.tensor_tensor(xb, xb, first.unsqueeze(1).to_broadcast([P, TB, E]), ALU.add)\
                        .then_inc(set_step, 1)
                    done += 1

            def scale_w2():
                for s_ in range(SETS):
                    part = w2[:, s_ * HC * E:(s_ + 1) * HC * E]
                    dve.tensor_scalar(part, part, coef_half[:, s_:s_ + 1], None, ALU.mult).then_inc(set_step, 1)

            evac_heads(1, H // 4)
            k_high(0, 0)
            dve.tensor_copy(y3, gb_bc[:, 2 * E:3 * E].unsqueeze(1).to_broadcast([P, NT, E])).then_inc(route, 1)
            evac_heads(H // 4, H // 4 + 1)
            weights()
            evac_heads(H // 4 + 1, H // 4 + 2)
            added()
            evac_heads(H // 4 + 2, H // 4 + 3)
            scale_w2()
            evac_heads(H // 4 + 3, H // 2)


            def row_max(g, k, s):
                m = (k % 2) * 2 + s
                dve.wait_ge(s_ready, 2 * (g * BODY + k) + s + 1)
                dve.tensor_reduce(neg_max[:, m:m + 1], slot[SLOT[2 * k + s]], AX.X, ALU.max, negate=True)\
                    .then_inc(max_done, 1)

            def step(g, k):
                kb, j = divmod(k, QB)
                m, km = g * BODY + k - 1, (k - 1) % BODY
                l, r, e = (km % 4) * 2, km * 2, km % 2
                if now(g, k):
                    row_max(g, k, 0)
                if now(g, k, 1):
                    dve.wait_ge(exp_done, 2 * m + 2)
                    dve.reciprocal(l_inv[:, r:r + 2], l_sum[:, l:l + 2]).then_inc(recip_done, 1)
                    dve.tensor_scalar(l1_neg[:, e:e + 1], l_sum[:, l:l + 1], lam_neg, None, ALU.mult)\
                        .then_inc(recip_done, 1)
                    dve.wait_ge(recip_done, 2 * m + 2)
                    e2 = e2_buf[:, km % 4 * S:(km % 4 + 1) * S]
                    dve.tensor_scalar(e2, e2, l_inv[:, r + 1:r + 2], l1_neg[:, e:e + 1], ALU.mult, ALU.mult)\
                        .then_inc(scaled, 1)
                if now(g, k):
                    row_max(g, k, 1)
                if k % TB == 1 and now(g, k, -TB):
                    k_high(g * 2 + k // TB + 1, (k // TB + 1) % 2)
                if j == 1 and now(g, k - j, 2 * QB):
                    dve.wait_ge(y_mm, g * (BODY // QB) + kb - 1)
                    tile0 = (g * 2 + kb // 2 - 1) // H * TB + (kb % 2) * QB
                    for t in range(QB):
                        tile = y_acc[:, bass.ds((tile0 + t) * E, E)]
                        r1 = (((kb - 2) * QB + t) % BODY) * 2
                        add = dve.scalar_tensor_tensor(out=tile, in0=o_ps[:, t * E:(t + 1) * E],
                                                       scalar=l_inv[:, r1:r1 + 1], in1=tile,
                                                       op0=ALU.mult, op1=ALU.add)
                    add.then_inc(y_evac, 1)

            def norm_y(part):
                half = part % 2
                tiles = slice(half * TB, (half + 1) * TB)
                yb = y3[:, tiles, :]

                def over_tokens(v):
                    return v[:, tiles].unsqueeze(2).to_broadcast([P, TB, E])

                if part in (0, 1):
                    dve.wait_ge(y_evac, STEPS // QB)
                    dve.tensor_reduce(sum_x[:, tiles], yb, AX.X, ALU.add).then_inc(lny, 1)
                    if half:
                        dve.wait_ge(lny, 2)
                        dve.tensor_scalar(mean_x, sum_x, 1.0 / E, None, ALU.mult).then_inc(lny, 1)
                elif part in (2, 3):
                    dve.wait_ge(lny, 3)
                    dve.tensor_tensor(yb, yb, over_tokens(mean_x), ALU.subtract).then_inc(lny, 1)
                elif part in (4, 5):
                    dve.wait_ge(lny, 4 + half)
                    dve.tensor_tensor(y_sq[:, tiles, :], yb, yb, ALU.mult).then_inc(lny, 1)
                elif part in (6, 7):
                    dve.wait_ge(lny, 6 + half)
                    dve.tensor_reduce(sum_x[:, tiles], y_sq[:, tiles, :], AX.X, ALU.add).then_inc(lny, 1)
                    if half:
                        dve.wait_ge(lny, 9)
                        dve.tensor_scalar(var_x, sum_x, 1.0 / E, LN_EPS, ALU.mult, ALU.add).then_inc(lny, 1)

            def finish_y(part):
                if part == 0:
                    dve.wait_ge(lny_sqrt, 1)
                    inv_std(slice(0, NT), lny, 10)
                elif part <= 3 * B:
                    b, what = divmod(part - 1, 3)
                    tiles = slice(b * TB, (b + 1) * TB)
                    yb = y3[:, tiles, :]
                    other = (rstd_x[:, tiles].unsqueeze(2).to_broadcast([P, TB, E]),
                             gb_bc[:, 0:E].unsqueeze(1).to_broadcast([P, TB, E]), x3[:, tiles, :])[what]
                    dve.wait_ge(lny, 13 + part)
                    dve.tensor_tensor(yb, yb, other, (ALU.mult, ALU.mult, ALU.add)[what]).then_inc(lny, 1)

            def sum_up(b):
                dve.wait_ge(lny, 17 + 3 * b)
                dve.wait_ge(out_mm, (b + 1) * UNITS // B)
                for quad in range(2):
                    bank = ps[:, (6 + quad) * BANK:(7 + quad) * BANK]
                    part = y_acc[:, (2 * b + quad) * BANK:(2 * b + quad + 1) * BANK]
                    dve.tensor_tensor(part, part, bank, ALU.add).then_inc(f_out, 1)

            def network(u):
                if u < UNITS:
                    t = t_buf[u % Z_BUFS]
                    dve.wait_ge(z_done, u + 1)
                    dve.tensor_scalar(t, t, GELU_A, 1.0, ALU.mult, ALU.add).then_inc(cubic, 1)
                if GELU_LAG <= u < UNITS + GELU_LAG:
                    v = u - GELU_LAG
                    z, t = z_buf[v % Z_BUFS], t_buf[v % Z_BUFS]
                    dve.wait_ge(tanh_done, v + 1)
                    after(dve, out_mm, v - 3)
                    dve.scalar_tensor_tensor(out=hidden[v % 4], in0=t, scalar=1.0, in1=z,
                                             op0=ALU.add, op1=ALU.mult).then_inc(h_done, 1)

            def start_network(k):
                if k in (3, 4):
                    network(k - 3)

            attention(dve, step, QB + 2, start_network)
            for u in range(2, UNITS + OUT_LAG):
                network(u)
                if u == 2:
                    norm_y(0)
                if u <= 8:
                    norm_y(u - 1)
                if u > SQRT_AT:
                    finish_y(u - SQRT_AT - 1)
                for b in range(B):
                    if u == (b + 1) * UNITS // B + OUT_LAG - 1:
                        sum_up(b)


_INS = ["L0_attn_X", "L0_attn_Wq", "L0_attn_bq", "L0_attn_Wk", "L0_attn_bk", "L0_attn_Wv", "L0_attn_bv",
        "L0_attn_Wo", "L0_attn_bo", "L0_attn_gamma", "L0_attn_beta", "L0_attn_lam", "L0_ffn_alpha",
        "L0_ffn_w_gate", "L0_ffn_b_gate", "L0_ffn_W1m", "L0_ffn_b1m", "L0_ffn_W2m", "L0_ffn_b2m",
        "L0_ffn_W1e", "L0_ffn_b1e", "L0_ffn_W2e", "L0_ffn_b2e"]


def kernel(**inputs):
    import numpy as np
    import concourse.bacc as bacc
    from concourse.bass_utils import run_bass_kernel_spmd

    nc = bacc.Bacc("TRN2", target_bir_lowering=False, num_devices=1)
    arrays, args = {}, []
    for name in _INS:
        a = np.asarray(inputs[name])
        if name in ("L0_attn_bq", "L0_attn_bk"):
            a = a.T
        elif name in ("L0_ffn_b1m", "L0_ffn_b1e"):
            a = np.swapaxes(a.reshape(a.shape[:-1] + (HC, P)), -1, -2)
        a = np.ascontiguousarray(a)
        arrays[f"in_{name}"] = a
        args.append(nc.dram_tensor(f"in_{name}", a.shape, mybir.dt.from_np(a.dtype), kind="ExternalInput").ap())
    args.append(nc.dram_tensor("out", (B, S, E), F32, kind="ExternalOutput").ap())
    build(nc, *args)
    r = run_bass_kernel_spmd(nc, [arrays], core_ids=[0])
    return r.results[0]["out"]
```

```python
from contextlib import ExitStack

import concourse.bass as bass
from concourse import mybir

F32 = mybir.dt.float32
F32R = mybir.dt.float32r
U32 = mybir.dt.uint32
ALU = mybir.AluOpType
ACT = mybir.ActivationFunctionType
AX = mybir.AxisListType

P = 128
B, S, E = 2, 1024, 128
H, D = 16, 64
TOK = B * S
NT = TOK // P
TB = S // P
IT = B * H
STEPS = IT * TB
QB = 4
KC = S // P
HID, NEXP, TOPK = 512, 8, 2
HC = HID // P
SETS = 1 + B * TOPK
LAG = 3
BANK = 512
UNITS = B * (1 + TOPK) * HC
SET_STEPS = 4 + 2 * SETS + 4 * B
OUT_LAG = 4
GELU_LAG = 2
Z_BUFS = 4
SQRT_AT = 10
BODY = 2 * TB
PROJ_AT = (2, 5)
SPLIT_W_AT = 5
PART_DMAS = 12
PV_AT = {(3, 0): 0, (3, 1): 2, (0, 0): 4, (0, 1): 6}
OUT_AT = (2, 0)
LN_EPS = 1e-5
OUT_SCALE = 0.2
QK_SCALE = 0.125
GELU_A, GELU_C = 0.044715, 0.7978845608028654


def build(nc, X, Wq, bq, Wk, bk, Wv, bv, Wo, bo, gamma, beta, lam,
          alpha, w_gate, b_gate, W1m, b1m, W2m, b2m, W1e, b1e, W2e, b2e, out):
    v_scratch = nc.dram_tensor("v_scratch", (NT, P, H * D), F32, kind="Internal").ap()
    gate_scratch = nc.dram_tensor("gate_scratch", (1, B * TOPK), F32, kind="Internal").ap()

    with ExitStack() as ctx:
        def sb(name, cols, dt=F32):
            return ctx.enter_context(nc.sbuf_tensor(name, [P, cols], dt))

        def sem(name):
            return ctx.enter_context(nc.semaphore(name))

        x_all = sb("x_all", NT * E)
        x3 = x_all[:, :].rearrange("p (t e) -> p t e", e=E)
        xT_hi = sb("xT_hi", TOK, F32R)
        xT_lo = sb("xT_lo", TOK, F32R)
        y_acc = sb("y_acc", NT * E)
        y3 = y_acc[:, :].rearrange("p (t e) -> p t e", e=E)
        wo_dup = sb("wo_dup", H * E)
        wo3 = wo_dup[:, :].rearrange("p (h e) -> p h e", e=E)
        work = sb("work", 8192)
        pt = sb("pt", 8192)
        q_st = sb("q_st", 2 * 2 * S, F32R)
        k_hi = sb("k_hi", 2 * 2 * S, F32R)
        k_lo = sb("k_lo", 2 * 2 * S, F32R)
        v_h = sb("v_h", 2 * KC * D)
        p_mix = sb("p_mix", 4 * S)
        o_t = sb("o_t", 2 * BANK)
        ident = sb("ident", P)
        w1_raw = sb("w1_raw", SETS * HID)
        w2 = sb("w2", SETS * HC * E)
        wqk_raw = sb("wqk_raw", 2 * P)
        wqk_hi = sb("wqk_hi", 2 * P, F32R)
        wqk_lo = sb("wqk_lo", 2 * P, F32R)
        qk_bias = sb("qk_bias", 4 * H)
        bk_in, bq_in = qk_bias[:, 0:H], qk_bias[:, H:2 * H]
        bias_of = qk_bias[:, 2 * H:4 * H]
        b1_col = sb("b1_col", SETS * HC)
        b2_bc = sb("b2_bc", SETS * E)
        gb_bc = sb("gb_bc", 3 * E)
        small = sb("small", 512)
        top_idx = sb("top_idx", 8, U32)

        sum_x, mean_x, var_x = (small[:, i * NT:(i + 1) * NT] for i in range(3))
        std_x, rstd_x, tmp_x = (small[:, i * NT:(i + 1) * NT] for i in range(3, 6))
        rowsum = small[:, 96:100]
        mean_tok = small[:, 100:102]
        lam_neg = small[:, 102:103]
        a_mix = small[:, 103:104]
        a_rest = small[:, 104:105]
        coef = small[:, 105:105 + SETS]
        coef_half = small[:, 110:110 + SETS]
        gates = small[:, 116:120]
        logit, prob = small[0:B, 120:128], small[0:B, 128:136]
        lg_max, lg_sum = small[0:B, 136:137], small[0:B, 137:138]
        top8 = small[0:B, 138:146]
        gate_w = small[0:B, 146:148]
        bg_bc = small[0:B, 148:156]
        neg_max = small[:, 160:164]
        l_sum = small[:, 164:172]
        l1_neg = small[:, 172:174]
        l_inv = small[:, 176:176 + 32]
        wg = small[:, 208:216]
        lam_in = small[:, 216:217]
        al_in = small[:, 217:218]
        bias_now = [small[:, 238 + 2 * i:240 + 2 * i] for i in range(2)]
        zero, eighth = small[:, 242:243], small[:, 243:244]

        part_hi, part_lo = ([work[:, (i + j) * S:(i + j + 1) * S] for i in (0, 2)] for j in range(2))
        e2_buf = work[:, 4 * S:8 * S]
        pt4 = pt[:, :].rearrange("p (n c q) -> p n c q", n=2, c=KC)
        qs4 = q_st[:, :].rearrange("p (n s t) -> p n s t", n=2, s=2)
        kh4 = k_hi[:, :].rearrange("p (n s t) -> p n s t", n=2, s=2)
        kl4 = k_lo[:, :].rearrange("p (n s t) -> p n s t", n=2, s=2)
        vh4 = v_h[:, :].rearrange("p (n c d) -> p n c d", n=2, c=KC)
        bv_bc = o_t[:, :]
        wv_raw = w1_raw[:, 0:H * D]
        wv_hi, wv_lo = k_hi[:, 2 * S:2 * S + H * D], k_lo[:, 2 * S:2 * S + H * D]
        v_st = pt[:, :].rearrange("p (t n) -> p t n", t=TB)
        w1_hi, w1_lo = ([t[:, i * HID:(i + 1) * HID] for i in range(SETS - 1)] for t in (q_st, k_hi))
        w1_hi.append(k_lo[:, 0:HID])
        w1_lo.append(k_lo[:, HID:2 * HID])
        hidden = [pt[:, i * S:(i + 1) * S] for i in range(4)]
        z_buf = [work[:, i * S:(i + 1) * S] for i in range(Z_BUFS)]
        t_buf = [work[:, (4 + i) * S:(5 + i) * S] for i in range(Z_BUFS)]
        y_sq = pt[:, 4 * S:6 * S].rearrange("p (t e) -> p t e", e=E)
        w1r3 = w1_raw[:, :].rearrange("p (s n) -> p s n", s=SETS)
        w24 = w2[:, :].rearrange("p (s c e) -> p s c e", s=SETS, c=HC)

        ps = ctx.enter_context(nc.psum_tensor("ps", [P, 8 * BANK], F32))
        slot = [ps[:, i * S:(i + 1) * S] for i in range(3)]
        pt_ps = ps[:, 6 * BANK:7 * BANK]
        o_ps = ps[:, 7 * BANK:8 * BANK]

        x_loaded = [sem(f"x_loaded{b}") for b in range(B)]
        small_loaded, bias_loaded = sem("small_loaded"), sem("bias_loaded")
        wv_loaded, wo_loaded, experts_loaded = sem("wv_loaded"), sem("wo_loaded"), sem("experts_loaded")
        id_ready, ln_step, sqrt_done = sem("id_ready"), sem("ln_step"), sem("sqrt_done")
        xn_ready, xt_ps, xt_hi, xt_lo = sem("xn_ready"), sem("xt_ps"), sem("xt_hi"), sem("xt_lo")
        wv_split, v_mm, v_evac = sem("wv_split"), sem("v_mm"), sem("v_evac")
        v_stored = [sem(f"v_stored{i}") for i in range(TB)]
        route, route_mm, route_act = sem("route"), sem("route_mm"), sem("route_act")
        gates_out, gates_in, set_step = sem("gates_out"), sem("gates_in"), sem("set_step")
        bias_table, bias_ready = sem("bias_table"), sem("bias_ready")
        w_loaded, w_split, proj_mm = sem("w_loaded"), sem("w_split"), sem("proj_mm")
        hi_done, lo_done, parts_loaded = sem("hi_done"), sem("lo_done"), sem("parts_loaded")
        v_loaded = [sem(f"v_loaded{i}") for i in range(2)]
        s_ready, max_done, exp_done = sem("s_ready"), sem("max_done"), sem("exp_done")
        recip_done = sem("recip_done")
        scaled, mix_done = sem("scaled"), sem("mix_done")
        pt_ready, pt_evac = sem("pt_ready"), sem("pt_evac")
        pv_done, o_evac, y_mm, y_evac = sem("pv_done"), sem("o_evac"), sem("y_mm"), sem("y_evac")
        w1_split, h_mm, z_done = sem("w1_split"), sem("h_mm"), sem("z_done")
        cubic, arg_done = sem("cubic"), sem("arg_done")
        tanh_done, h_done, out_mm, f_out = sem("tanh_done"), sem("h_done"), sem("out_mm"), sem("f_out")
        y_started, lny, lny_sqrt = sem("y_started"), sem("lny"), sem("lny_sqrt")
        stored = sem("stored")

        def after(eng, s, count):
            if not isinstance(count, int) or count > 0:
                eng.wait_ge(s, count)

        def now(g, k, lag=0):
            return not isinstance(g, int) or 0 <= g * BODY + k - lag < STEPS

        def attention(eng, step, lag, beside=None):
            for k in range(BODY):
                step(0, k)
            with eng.Fori(1, STEPS // BODY - 1) as g:
                for k in range(BODY):
                    step(g, k)
            for k in range(BODY):
                step(STEPS // BODY - 1, k)
            for k in range(lag):
                step(STEPS // BODY, k)
                if beside:
                    beside(k)

        TILES = []
        for k in range(BODY):
            TILES += [(k, 0), (k, 1)] + [(k, "proj")] * (k % TB in PROJ_AT)
        SLOT = {tile: n % 3 for n, tile in enumerate(TILES)}
        assert len(TILES) % 3 == 0

        def slot_free(g, tile):
            n = TILES.index(tile) - 3
            g, (k, what) = (g, TILES[n]) if n >= 0 else (g - 1, TILES[n])
            if isinstance(g, int) and (g < 0 or (what == "proj" and not now(g, k, -TB))):
                return None
            if what == "proj":
                return lo_done, 2 * (2 * g + k // TB) + 3 + PROJ_AT.index(k % TB)
            return exp_done, 2 * (g * BODY + k) + what + 1

        block = ctx.enter_context(nc.Block())

        @block.sync
        def _(sp):
            xv = X.rearrange("b (t p) e -> p (b t) e", p=P)
            for b in range(B):
                sp.dma_start(x3[:, b * TB:(b + 1) * TB, :], xv[:, b * TB:(b + 1) * TB, :]).then_inc(x_loaded[b], 16)
            sp.dma_start(wv_raw.rearrange("p (h d) -> p h d", h=H), Wv.rearrange("h e d -> e h d"))\
                .then_inc(wv_loaded, 16)
            sp.dma_start(bv_bc, bv.rearrange("h d -> (h d)").partition_broadcast(P)).then_inc(bias_loaded, 16)
            for i, v in enumerate((gamma, beta, bo)):
                sp.dma_start(gb_bc[:, i * E:(i + 1) * E], v.partition_broadcast(P)).then_inc(bias_loaded, 16)
            for half in range(2):
                sp.dma_start(wo3[half * D:(half + 1) * D, :, :], Wo.rearrange("(h d) e -> d h e", d=D))\
                    .then_inc(wo_loaded, 16)

            def load_set(s_, w1, b1, w2_, b2):
                sp.dma_start(w1r3[:, s_, :], w1).then_inc(experts_loaded, 16)
                sp.dma_start(w24[:, s_, :, :], w2_.rearrange("(c p) e -> p c e", p=P)).then_inc(experts_loaded, 16)
                sp.dma_start(b1_col[:, s_ * HC:(s_ + 1) * HC], b1).then_inc(experts_loaded, 16)
                sp.dma_start(b2_bc[:, s_ * E:(s_ + 1) * E], b2.partition_broadcast(P)).then_inc(experts_loaded, 16)

            sp.wait_ge(wv_split, 2)
            load_set(0, W1m, b1m, W2m, b2m)

            def lay_out(par, w):
                for s_ in range(2):
                    src = slice(s_ * D, (s_ + 1) * D)
                    for part, kept in ((part_hi[w], kh4), (part_lo[w], kl4)):
                        if w == 0:
                            halves = ((kept, 0), (kept, 1))
                        else:
                            halves = ((qs4, 0 if kept is kh4 else 1),)
                        for dst, half in halves:
                            sp.dma_start(dst[half * D:(half + 1) * D, par, s_, :].bitcast(F32), part[src, :])\
                                .then_inc(parts_loaded, 16)

            def load_v(b, h, par):
                sp.dma_start(v_h[:, par * KC * D:(par + 1) * KC * D].rearrange("p (c d) -> p c d", d=D),
                             v_scratch.rearrange("(b c) p (h d) -> b h p c d", b=B, d=D)
                             [bass.ds(b, 1), bass.ds(h, 1), :, :, :].rearrange("o u p c d -> (o u p) c d"))\
                    .then_inc(v_loaded[par], 16)

            def load_w(h):
                for w, src in enumerate((Wk, Wq)):
                    sp.dma_start(wqk_raw[:, w * P:(w + 1) * P],
                                 src[bass.ds(h, 1), :, :].rearrange("o e c -> (o e) c")).then_inc(w_loaded, 16)

            for w in range(2):
                sp.wait_ge(lo_done, w + 1)
                lay_out(0, w)
            sp.wait_ge(w_split, 3)
            load_w(1)

            for i in range(NT):
                sp.wait_ge(v_evac, 2 * i + 2)
                sp.dma_start(v_scratch[i, :, :], v_st[:, i % TB, :]).then_inc(v_stored[i % TB], 16)
            sp.wait_ge(w_split, 6)
            load_w(2)

            sp.wait_ge(route, 14)
            sp.dma_start(gate_scratch.rearrange("o (b k) -> (o b) k", b=B), gate_w).then_inc(gates_out, 16)
            for b in range(B):
                for c in range(TOPK):
                    e = sp.value_load(top_idx[b:b + 1, c:c + 1], min_val=0, max_val=NEXP - 1)
                    load_set(1 + TOPK * b + c, W1e[bass.ds(e, 1), :, :].rearrange("o a n -> (o a) n"),
                             b1e[bass.ds(e, 1), :, :].rearrange("o p c -> (o p) c"),
                             W2e[bass.ds(e, 1), :, :].rearrange("o n e -> (o n) e"),
                             b2e[bass.ds(e, 1), :].rearrange("o n -> (o n)"))
            sp.wait_ge(gates_out, 16)
            sp.dma_start(gates, gate_scratch.rearrange("o n -> (o n)").partition_broadcast(P))\
                .then_inc(gates_in, 16)

            for v in v_stored:
                sp.wait_ge(v, 16 * B)
            load_v(0, 0, 0)

            def prepare(b, n, par):
                h, next_h = n - b * H, (n + 2) % H if isinstance(n, int) else n + 2 - b * H
                after(sp, pv_done, 2 * n - 2)
                load_v(b, h, par)
                sp.wait_ge(lo_done, 2 * n + 1)
                lay_out(par, 0)
                sp.wait_ge(lo_done, 2 * n + 2)
                lay_out(par, 1)
                if isinstance(n, int) and n + 2 >= IT:
                    return
                sp.wait_ge(w_split, 3 * n + 6)
                load_w(next_h)

            prepare(0, 1, 1)
            for b in range(B):
                with sp.Fori(b * H // 2 + (b == 0), (b + 1) * H // 2 - 1) as g:
                    for par in range(2):
                        prepare(b, 2 * g + par, par)
                for par in range(2):
                    prepare(b, (b + 1) * H - 2 + par, par)

            ov = out.rearrange("b (t p) e -> p (b t) e", p=P)
            for i in range(NT // 4):
                sp.wait_ge(f_out, i + 1)
                sp.dma_start(ov[:, 4 * i:4 * i + 4, :], y3[:, 4 * i:4 * i + 4, :]).then_inc(stored, 16)
            sp.wait_ge(stored, 16 * NT // 4)

        @block.gpsimd
        def _(pool):
            pool.memset(ident[:, :], 0.0).then_inc(id_ready, 1)
            pool.wait_ge(id_ready, 1)
            pool.affine_select(out=ident[:, :], in_=ident[:, :], compare_op=ALU.not_equal, fill=1.0,
                               base=0, pattern=[[-1, P]], channel_multiplier=1).then_inc(id_ready, 1)
            pool.dma_start(wg, w_gate).then_inc(small_loaded, 16)
            pool.dma_start(bg_bc, b_gate.partition_broadcast(B)).then_inc(small_loaded, 16)
            pool.dma_start(lam_in, lam.partition_broadcast(P)).then_inc(small_loaded, 16)
            pool.dma_start(al_in, alpha.partition_broadcast(P)).then_inc(small_loaded, 16)

            pool.memset(zero, 0.0).then_inc(id_ready, 1)
            pool.memset(eighth, QK_SCALE).then_inc(id_ready, 1)

            pool.wait_ge(wv_loaded, 16)
            pool.tensor_copy(wv_hi, wv_raw).then_inc(wv_split, 1)
            pool.wait_ge(wv_split, 1)
            pool.tensor_tensor(wv_lo, wv_raw, wv_hi.bitcast(F32), ALU.subtract).then_inc(wv_split, 1)

            def split_w(n):
                pool.wait_ge(w_loaded, 32 * (n + 1))
                pool.tensor_tensor(wqk_raw[:, P:2 * P], wqk_raw[:, P:2 * P], eighth.to_broadcast([P, P]), ALU.mult)\
                    .then_inc(w_split, 1)
                after(pool, proj_mm, 2 * n)
                pool.wait_ge(w_split, 3 * n + 1)
                pool.tensor_tensor(wqk_hi[:, :], wqk_raw[:, :], zero.to_broadcast([P, 2 * P]), ALU.subtract)\
                    .then_inc(w_split, 1)
                pool.wait_ge(w_split, 3 * n + 2)
                pool.tensor_tensor(wqk_lo[:, :], wqk_raw[:, :], wqk_hi[:, :].bitcast(F32), ALU.subtract)\
                    .then_inc(w_split, 1)

            def start_y():
                pool.wait_ge(bias_loaded, 96)
                pool.tensor_copy(y3, gb_bc[:, 2 * E:3 * E].unsqueeze(1).to_broadcast([P, NT, E]))\
                    .then_inc(y_started, 1)

            bias = b2_bc[:, :].rearrange("p (s e) -> p s e", s=SETS)

            def set_weights():
                pool.wait_ge(gates_in, 16)
                pool.tensor_scalar(coef[:, 1:SETS], gates, a_rest, None, ALU.mult).then_inc(set_step, 1)
                pool.tensor_copy(coef[:, 0:1], a_mix).then_inc(set_step, 1)
                pool.wait_ge(set_step, 2)
                pool.tensor_scalar(coef_half, coef, 0.5, None, ALU.mult).then_inc(set_step, 1)
                pool.tensor_scalar(gb_bc[:, 0:2 * E], gb_bc[:, 0:2 * E], OUT_SCALE, None, ALU.mult)\
                    .then_inc(set_step, 1)
                pool.wait_ge(experts_loaded, 64 * SETS)
                for s_ in range(SETS):
                    pool.tensor_scalar(bias[:, s_, :], bias[:, s_, :], coef[:, s_:s_ + 1], None, ALU.mult)\
                        .then_inc(set_step, 1)

            def add_biases(b):
                done = 4 + SETS + 4 * b
                first = bias[:, 1 + TOPK * b, :]
                for v in (bias[:, 2 + TOPK * b, :], bias[:, 0, :], gb_bc[:, E:2 * E]):
                    pool.wait_ge(set_step, done)
                    pool.tensor_tensor(first, first, v, ALU.add).then_inc(set_step, 1)
                    done += 1
                pool.wait_ge(set_step, done)
                xb = x3[:, b * TB:(b + 1) * TB, :]
                pool.tensor_tensor(xb, xb, first.unsqueeze(1).to_broadcast([P, TB, E]), ALU.add)\
                    .then_inc(set_step, 1)

            def scale_w2(s_):
                part = w2[:, s_ * HC * E:(s_ + 1) * HC * E]
                pool.tensor_scalar(part, part, coef_half[:, s_:s_ + 1], None, ALU.mult).then_inc(set_step, 1)

            pool.wait_ge(id_ready, 4)
            split_w(0)
            start_y()
            split_w(1)

            def step(g, k):
                n = g * BODY + k
                if now(g, k, 1):
                    e1 = p_mix[:, (k - 1) % 4 * S:((k - 1) % 4 + 1) * S]
                    e2 = e2_buf[:, (k - 1) % 4 * S:((k - 1) % 4 + 1) * S]
                    pool.wait_ge(scaled, n)
                    pool.tensor_tensor(e1, e1, e2, ALU.add).then_inc(mix_done, 1)
                if k % TB == SPLIT_W_AT and now(g, k, -2 * TB):
                    split_w(g * 2 + k // TB + 2)
                if isinstance(g, int) and g == 0:
                    if k == 6:
                        set_weights()
                    if 7 <= k < 7 + B:
                        add_biases(k - 7)
                    if 7 + B <= k < 7 + B + SETS:
                        scale_w2(k - 7 - B)
                s_ = k - TB - 1
                if isinstance(g, int) and g == STEPS // BODY - 1 and 0 <= s_ < SETS:
                    pool.wait_ge(s_ready, 2 * TB * (IT - 1))
                    pool.tensor_tensor(w1_hi[s_], w1r3[:, s_, :], zero.to_broadcast([P, HID]), ALU.subtract)\
                        .then_inc(w1_split, 1)
                    pool.wait_ge(w1_split, 2 * s_ + 1)
                    pool.tensor_tensor(w1_lo[s_], w1r3[:, s_, :], w1_hi[s_].bitcast(F32), ALU.subtract)\
                        .then_inc(w1_split, 1)

            attention(pool, step, 1)

            for u in range(UNITS):
                z, t = z_buf[u % Z_BUFS], t_buf[u % Z_BUFS]
                pool.wait_ge(cubic, u + 1)
                pool.tensor_tensor(t, t, z, ALU.mult).then_inc(arg_done, 1)

        @block.tensor
        def _(pe):
            pe.wait_ge(id_ready, 2)
            def turn_x(b):
                pe.wait_ge(xn_ready, b + 1)
                for i in range(b * TB, (b + 1) * TB):
                    mm = pe.transpose(ps[:, i * P:(i + 1) * P], p_mix[:, i * E:(i + 1) * E], ident[:, :])
                    if i % 4 == 3:
                        mm.then_inc(xt_ps, 1)

            def proj(n, w, into):
                t0 = n // H * S
                pe.wait_ge(w_split, 3 * n + 3)
                for j, (wt, a) in enumerate(((wqk_hi, xT_hi), (wqk_lo, xT_hi), (wqk_hi, xT_lo))):
                    for half in range(2):
                        mm = pe.matmul(into[:, half * BANK:(half + 1) * BANK], wt[:, w * P:(w + 1) * P],
                                       a[:, bass.ds(t0 + half * BANK, BANK)], start=j == 0, stop=j == 2)
                mm.then_inc(proj_mm, 1)

            turn_x(0)
            pe.wait_ge(xt_lo, 2)
            proj(0, 0, slot[0])
            proj(0, 1, slot[2])
            turn_x(1)
            pe.wait_ge(wv_split, 2)
            for i in range(NT):
                for hv in range(2):
                    u = 2 * i + hv
                    bank = 4 + (u + 2) % 4
                    if u == 2:
                        pe.wait_ge(lo_done, 2)
                    if u % 8 == 0:
                        pe.wait_ge(xt_lo, i // 4 + 1)
                    if u == 10:
                        pe.wait_ge(route, 2)
                        pe.wait_ge(small_loaded, 64)
                        pe.matmul(ps[0:B, 2 * BANK:2 * BANK + NEXP], mean_tok, wg, start=True, stop=True)\
                            .then_inc(route_mm, 1)
                    after(pe, v_evac, u - 3)
                    for j, (a, w) in enumerate(((xT_hi, wv_hi), (xT_lo, wv_hi), (xT_hi, wv_lo))):
                        mm = pe.matmul(ps[:, bank * BANK:(bank + 1) * BANK], a[:, i * P:(i + 1) * P],
                                       w[:, hv * BANK:(hv + 1) * BANK], start=j == 0, stop=j == 2)
                    mm.then_inc(v_mm, 1)

            pe.wait_ge(v_evac, 2 * NT)

            def scores(g, k, s):
                tile = (k, s)
                free = slot_free(g, tile)
                if free:
                    pe.wait_ge(*free)
                par, q0 = k // TB, (k % TB) * P
                for j, kk in enumerate((kh4, kl4)):
                    for half in range(2):
                        cols = slice(half * BANK, (half + 1) * BANK)
                        mm = pe.matmul(slot[SLOT[tile]][:, cols], qs4[:, par, s, q0:q0 + P], kk[:, par, s, cols],
                                       start=j == 0, stop=j == 1)
                mm.then_inc(s_ready, 1)

            def turn(g, k, half):
                n = g * BODY + k - LAG
                if half == 0:
                    pe.wait_ge(mix_done, n + 1)
                after(pe, pt_evac, 2 * n + half)
                for c in range(4):
                    col = (k - LAG) % 4 * S + (half * 4 + c) * P
                    mm = pe.transpose(pt_ps[:, c * P:(c + 1) * P], p_mix[:, col:col + P], ident[:, :])
                mm.then_inc(pt_ready, 1)

            def pv(g, kb, c0):
                blk = g * (BODY // QB) + kb
                if c0 == 0:
                    pe.wait_ge(pt_evac, 2 * QB * (blk + 1))
                    after(pe, y_evac, blk)
                    if kb % 2 == 0:
                        pe.wait_ge(v_loaded[kb // 2], 16 * (g + 1))
                for c in (c0, c0 + 1):
                    half = c % 2
                    mm = pe.matmul(o_ps[half * D:(half + 1) * D, :], vh4[:, (kb // 2) % 2, c, :],
                                   pt4[:, kb % 2, c, :], start=c < 2, stop=c >= KC - 2,
                                   skip_group_check=True)
                if c0 == KC - 2:
                    mm.then_inc(pv_done, 1)

            def out_proj(g, kb):
                head = (g * 2 + kb // 2 - 1) % H
                pe.wait_ge(o_evac, g * (BODY // QB) + kb - 1)
                for t in range(QB):
                    col = (kb % 2) * BANK + t * P
                    mm = pe.matmul(o_ps[:, t * E:(t + 1) * E], o_t[:, col:col + P],
                                   wo_dup[:, bass.ds(head * E, E)], start=True, stop=True, skip_group_check=True)
                mm.then_inc(y_mm, 1)

            def values(g, k, half):
                kb, j = divmod(k, QB)
                back = 1 if j == 3 else 2
                if (j, half) in PV_AT and now(g, k - j, back * QB):
                    pv(g, kb - back, PV_AT[j, half])
                if (j, half) == OUT_AT and now(g, k - j, 2 * QB):
                    out_proj(g, kb)

            def step(g, k):
                kb, j = divmod(k, QB)
                if now(g, k):
                    if k % TB == 0:
                        pe.wait_ge(parts_loaded, 16 * PART_DMAS * (g * 2 + k // TB + 1))
                    scores(g, k, 0)
                if now(g, k, LAG):
                    turn(g, k, 0)
                values(g, k, 0)
                if now(g, k):
                    scores(g, k, 1)
                if now(g, k, LAG):
                    turn(g, k, 1)
                values(g, k, 1)
                if k % TB in PROJ_AT and now(g, k, -TB):
                    free = slot_free(g, (k, "proj"))
                    if free:
                        pe.wait_ge(*free)
                    proj(g * 2 + k // TB + 1, PROJ_AT.index(k % TB), slot[SLOT[k, "proj"]])


            def hidden_mm(u):
                b, i = divmod(u, (1 + TOPK) * HC)
                f, c = divmod(i, HC)
                set_ = 0 if f == 0 else TOPK * b + f
                after(pe, z_done, u - 2)
                for j, (w, a) in enumerate(((w1_hi, xT_hi), (w1_lo, xT_hi), (w1_hi, xT_lo))):
                    for half in range(2):
                        t0 = b * S + half * BANK
                        mm = pe.matmul(slot[u % 3][:, half * BANK:(half + 1) * BANK],
                                       w[set_][:, c * P:(c + 1) * P],
                                       a[:, t0:t0 + BANK], start=j == 0, stop=j == 2)
                mm.then_inc(h_mm, 1)

            def output_mm(u):
                b, i = divmod(u, (1 + TOPK) * HC)
                f, c = divmod(i, HC)
                pe.wait_ge(h_done, u + 1)
                if i == 0:
                    after(pe, f_out, 2 * b)
                for t in range(TB):
                    out_ps = ps[:, 6 * BANK + t * E:6 * BANK + (t + 1) * E]
                    mm = pe.matmul(out_ps, hidden[u % 4][:, t * P:(t + 1) * P],
                                   w24[:, 0 if f == 0 else TOPK * b + f, c, :],
                                   start=i == 0 and t % 4 == 0, stop=i == (1 + TOPK) * HC - 1,
                                   skip_group_check=True)
                mm.then_inc(out_mm, 1)

            def start_hidden(k):
                if k == 1:
                    pe.wait_ge(exp_done, 2 * STEPS)
                    pe.wait_ge(w1_split, 2 * SETS)
                if 1 <= k <= OUT_LAG:
                    hidden_mm(k - 1)

            pe.wait_ge(wo_loaded, 32)
            attention(pe, step, QB + 3, start_hidden)

            switch = UNITS // B + OUT_LAG
            for u in range(OUT_LAG, UNITS + OUT_LAG):
                if u < UNITS and u != switch + 1:
                    hidden_mm(u)
                if u == switch:
                    hidden_mm(u + 1)
                if u == OUT_LAG:
                    pe.wait_ge(y_evac, STEPS // QB)
                    pe.wait_ge(set_step, SET_STEPS)
                if u >= OUT_LAG:
                    output_mm(u - OUT_LAG)

        @block.scalar
        def _(act):
            act.dma_start(bq_in, bq).then_inc(bias_loaded, 16)
            act.dma_start(bk_in, bk).then_inc(bias_loaded, 16)
            for w, src in enumerate((Wk, Wq)):
                act.dma_start(wqk_raw[:, w * P:(w + 1) * P], src[0, :, :]).then_inc(w_loaded, 16)
            def high_x(i):
                act.wait_ge(xt_ps, i + 1)
                act.activation(xT_hi[:, i * BANK:(i + 1) * BANK], ps[:, i * BANK:(i + 1) * BANK], ACT.Copy,
                               accum_out=rowsum[:, i:i + 1]).then_inc(xt_hi, 1)

            for b in range(B):
                act.wait_ge(ln_step, 10 * b + 6)
                act.activation(std_x[:, b * TB:(b + 1) * TB], var_x[:, b * TB:(b + 1) * TB], ACT.Sqrt)\
                    .then_inc(sqrt_done, 1)
                if b == 0:
                    high_x(0)
                    high_x(1)
            act.wait_ge(bias_loaded, 96)
            bias3 = bias_of.rearrange("p (h w) -> p h w", w=2)
            act.activation(bias3[:, :, 0], bk_in, ACT.Copy).then_inc(bias_table, 1)
            act.mul(bias3[:, :, 1], bq_in, QK_SCALE).then_inc(bias_table, 1)
            act.wait_ge(bias_table, 2)

            def next_bias(n, par):
                act.activation(bias_now[par], bias_of[:, bass.ds(n % H * 2, 2)], ACT.Copy).then_inc(bias_ready, 1)

            def high_part(n, par, w, tile):
                act.wait_ge(bias_ready, n + 1)
                after(act, parts_loaded, 16 * PART_DMAS * n)
                act.wait_ge(proj_mm, 2 * n + 1 + w)
                act.activation(part_hi[w].bitcast(F32R), tile, ACT.Identity, bias=bias_now[par][:, w:w + 1],
                               scale=1.0).then_inc(hi_done, 1)

            next_bias(0, 0)
            high_part(0, 0, 0, slot[0])
            high_part(0, 0, 1, slot[2])
            high_x(2)
            high_x(3)
            act.wait_ge(route, 5)
            act.activation(prob, logit, ACT.Exp, bias=lg_max, scale=1.0, accum_out=lg_sum).then_inc(route_act, 1)


            def exps(g, k, s):
                n = g * BODY + k
                act.wait_ge(max_done, 2 * n + s + 1)
                if s == 0:
                    after(act, pt_ready, 2 * (n - 3))
                else:
                    after(act, mix_done, n - 3)
                m, l = (k % 2) * 2 + s, (k % 4) * 2 + s
                act.activation((p_mix, e2_buf)[s][:, k % 4 * S:(k % 4 + 1) * S], slot[SLOT[k, s]], ACT.Exp,
                               bias=neg_max[:, m:m + 1], scale=1.0, accum_out=l_sum[:, l:l + 1])\
                    .then_inc(exp_done, 1)

            def evac_pt(g, k, half):
                kb, j = divmod(k - LAG, QB)
                if half == 0 and isinstance(g, int) and g * BODY + k == LAG:
                    for v in v_stored:
                        act.wait_ge(v, 16 * B)
                if half == 0 and j == 0:
                    after(act, pv_done, g * (BODY // QB) + kb - 1)
                act.wait_ge(pt_ready, 2 * (g * BODY + k - LAG) + half + 1)
                act.activation(pt4[:, kb % 2, half * 4:half * 4 + 4, j * P:(j + 1) * P],
                               pt_ps.rearrange("p (c q) -> p c q", c=4), ACT.Copy).then_inc(pt_evac, 1)

            def step(g, k):
                kb, j = divmod(k, QB)
                if j == 1 and now(g, k - j, 2 * QB):
                    act.wait_ge(pv_done, g * (BODY // QB) + kb - 1)
                    act.activation(o_t[:, (kb % 2) * BANK:(kb % 2 + 1) * BANK], o_ps, ACT.Copy).then_inc(o_evac, 1)
                if now(g, k, LAG):
                    evac_pt(g, k, 0)
                if now(g, k):
                    exps(g, k, 0)
                if now(g, k, LAG):
                    evac_pt(g, k, 1)
                if now(g, k):
                    exps(g, k, 1)
                n, par = g * 2 + k // TB + 1, (k // TB + 1) % 2
                if k % TB == 0 and now(g, k, -TB):
                    next_bias(n, par)
                if k % TB in PROJ_AT and now(g, k, -TB):
                    high_part(n, par, PROJ_AT.index(k % TB), slot[SLOT[k, "proj"]])

            def gelu(u):
                if u == SQRT_AT:
                    act.wait_ge(lny, 10)
                    act.activation(std_x, var_x, ACT.Sqrt).then_inc(lny_sqrt, 1)
                if u < UNITS:
                    b, i = divmod(u, (1 + TOPK) * HC)
                    f, c = divmod(i, HC)
                    col = (0 if f == 0 else TOPK * b + f) * HC + c
                    z, t = z_buf[u % Z_BUFS], t_buf[u % Z_BUFS]
                    act.wait_ge(h_mm, u + 1)
                    if u < Z_BUFS:
                        act.wait_ge(mix_done, STEPS - Z_BUFS + u + 1)
                    after(act, h_done, u - Z_BUFS + 1)
                    act.activation(z, slot[u % 3], ACT.Identity, bias=b1_col[:, col:col + 1], scale=1.0)
                    act.activation(t, slot[u % 3], ACT.Square, bias=b1_col[:, col:col + 1], scale=1.0)\
                        .then_inc(z_done, 1)
                if u >= GELU_LAG:
                    t = t_buf[(u - GELU_LAG) % Z_BUFS]
                    act.wait_ge(arg_done, u - GELU_LAG + 1)
                    act.activation(t, t, ACT.Tanh, scale=GELU_C).then_inc(tanh_done, 1)

            def start_gelu(k):
                if k == 2:
                    act.wait_ge(set_step, SET_STEPS)
                if 2 <= k <= 4:
                    gelu(k - 2)

            attention(act, step, QB + 3, start_gelu)
            for u in range(3, UNITS + GELU_LAG):
                gelu(u)

        @block.vector
        def _(dve):
            xn3 = p_mix[:, 0:2 * S].rearrange("p (t e) -> p t e", e=E)
            sq3 = work[:, 0:S].rearrange("p (t e) -> p t e", e=E)

            def inv_std(t, s, base):
                dve.reciprocal(rstd_x[:, t], std_x[:, t]).then_inc(s, 1)
                dve.wait_ge(s, base + 1)
                dve.tensor_tensor(tmp_x[:, t], rstd_x[:, t], rstd_x[:, t], ALU.mult).then_inc(s, 1)
                dve.wait_ge(s, base + 2)
                dve.scalar_tensor_tensor(out=tmp_x[:, t], in0=tmp_x[:, t], scalar=-0.5, in1=var_x[:, t],
                                         op0=ALU.mult, op1=ALU.mult).then_inc(s, 1)
                dve.wait_ge(s, base + 3)
                dve.scalar_tensor_tensor(out=rstd_x[:, t], in0=tmp_x[:, t], scalar=1.5, in1=rstd_x[:, t],
                                         op0=ALU.add, op1=ALU.mult).then_inc(s, 1)

            def low_x(i):
                dve.wait_ge(xt_hi, i + 1)
                dve.tensor_tensor(xT_lo[:, i * BANK:(i + 1) * BANK], ps[:, i * BANK:(i + 1) * BANK],
                                  xT_hi[:, i * BANK:(i + 1) * BANK].bitcast(F32), ALU.subtract).then_inc(xt_lo, 1)

            for b in range(B):
                t = slice(b * TB, (b + 1) * TB)
                o = 10 * b
                dve.wait_ge(x_loaded[b], 16)
                dve.tensor_reduce(sum_x[:, t], x3[:, t, :], AX.X, ALU.add).then_inc(ln_step, 1)
                dve.wait_ge(ln_step, o + 1)
                dve.tensor_scalar(mean_x[:, t], sum_x[:, t], 1.0 / E, None, ALU.mult).then_inc(ln_step, 1)
                dve.wait_ge(ln_step, o + 2)
                dve.tensor_tensor(xn3[:, t, :], x3[:, t, :],
                                  mean_x[:, t].unsqueeze(2).to_broadcast([P, TB, E]), ALU.subtract)\
                    .then_inc(ln_step, 1)
                dve.wait_ge(ln_step, o + 3)
                dve.tensor_tensor(sq3, xn3[:, t, :], xn3[:, t, :], ALU.mult).then_inc(ln_step, 1)
                dve.wait_ge(ln_step, o + 4)
                dve.tensor_reduce(sum_x[:, t], sq3, AX.X, ALU.add).then_inc(ln_step, 1)
                dve.wait_ge(ln_step, o + 5)
                dve.tensor_scalar(var_x[:, t], sum_x[:, t], 1.0 / E, LN_EPS, ALU.mult, ALU.add)\
                    .then_inc(ln_step, 1)
                if b == 1:
                    low_x(0)
                    low_x(1)
                dve.wait_ge(sqrt_done, b + 1)
                inv_std(t, ln_step, o + 6)
                dve.wait_ge(ln_step, o + 10)
                dve.tensor_tensor(xn3[:, t, :], xn3[:, t, :],
                                  rstd_x[:, t].unsqueeze(2).to_broadcast([P, TB, E]), ALU.mult)\
                    .then_inc(xn_ready, 1)
            def low_part(n, par, w, tile):
                dve.wait_ge(hi_done, 2 * n + 1 + w)
                dve.scalar_tensor_tensor(out=part_lo[w].bitcast(F32R), in0=tile, scalar=bias_now[par][:, w:w + 1],
                                         in1=part_hi[w], op0=ALU.add, op1=ALU.subtract).then_inc(lo_done, 1)

            def evac_v(first, end):
                for u in range(first, end):
                    i, hv = divmod(u, 2)
                    bank = 4 + (u + 2) % 4
                    dve.wait_ge(v_mm, u + 1)
                    if hv == 0:
                        after(dve, v_stored[i % TB], 16 * (i // TB))
                    dve.tensor_tensor(v_st[:, i % TB, hv * BANK:(hv + 1) * BANK],
                                      ps[:, bank * BANK:(bank + 1) * BANK],
                                      bv_bc[:, hv * BANK:(hv + 1) * BANK], ALU.add).then_inc(v_evac, 1)

            low_part(0, 0, 0, slot[0])
            low_part(0, 0, 1, slot[2])
            low_x(2)
            low_x(3)
            dve.tensor_tensor(mean_tok, rowsum[:, 0:4:2], rowsum[:, 1:4:2], ALU.add).then_inc(route, 1)
            dve.wait_ge(route, 1)
            dve.tensor_scalar(mean_tok, mean_tok, 1.0 / S, None, ALU.mult).then_inc(route, 1)
            dve.wait_ge(bias_loaded, 96)
            evac_v(0, 8)
            dve.wait_ge(route_mm, 1)
            dve.tensor_tensor(logit, ps[0:B, 2 * BANK:2 * BANK + NEXP], bg_bc, ALU.add).then_inc(route, 1)
            dve.wait_ge(route, 3)
            dve.tensor_reduce(lg_max, logit, AX.X, ALU.max, negate=True).then_inc(route, 1)
            dve.tensor_scalar(a_mix, al_in, 0.1, 1.0, ALU.max, ALU.min).then_inc(route, 1)
            evac_v(8, 16)
            dve.wait_ge(route_act, 1)
            dve.reciprocal(lg_sum, lg_sum).then_inc(route, 1)
            dve.wait_ge(route, 6)
            dve.tensor_scalar(prob, prob, lg_sum, None, ALU.mult).then_inc(route, 1)
            dve.wait_ge(route, 7)
            dve.max(top8, prob).then_inc(route, 1)
            dve.wait_ge(route, 8)
            dve.max_index(top_idx[0:B, :], top8, prob).then_inc(route, 1)
            dve.tensor_tensor(lg_sum, top8[:, 0:1], top8[:, 1:2], ALU.add).then_inc(route, 1)
            dve.wait_ge(route, 10)
            dve.reciprocal(lg_sum, lg_sum).then_inc(route, 1)
            dve.wait_ge(route, 11)
            dve.tensor_scalar(gate_w, top8[:, 0:TOPK], lg_sum, None, ALU.mult).then_inc(route, 1)
            dve.tensor_scalar(lam_neg, lam_in, -1.0, None, ALU.mult).then_inc(route, 1)
            dve.tensor_scalar(a_rest, a_mix, -1.0, 1.0, ALU.mult, ALU.add).then_inc(route, 1)

            evac_v(16, 2 * NT)


            def row_max(g, k, s):
                m = (k % 2) * 2 + s
                dve.wait_ge(s_ready, 2 * (g * BODY + k) + s + 1)
                dve.tensor_reduce(neg_max[:, m:m + 1], slot[SLOT[k, s]], AX.X, ALU.max, negate=True)\
                    .then_inc(max_done, 1)

            def add_y(g, kb):
                if isinstance(g, int) and g == 0 and kb == 2:
                    dve.wait_ge(y_started, 1)
                dve.wait_ge(y_mm, g * (BODY // QB) + kb - 1)
                tile0 = (g * 2 + kb // 2 - 1) // H * TB + (kb % 2) * QB
                for t in range(QB):
                    tile = y_acc[:, bass.ds((tile0 + t) * E, E)]
                    r1 = (((kb - 2) * QB + t) % BODY) * 2
                    add = dve.scalar_tensor_tensor(out=tile, in0=o_ps[:, t * E:(t + 1) * E],
                                                   scalar=l_inv[:, r1:r1 + 1], in1=tile,
                                                   op0=ALU.mult, op1=ALU.add)
                add.then_inc(y_evac, 1)

            def step(g, k):
                kb, j = divmod(k, QB)
                m, km = g * BODY + k - 1, (k - 1) % BODY
                l, r, e = (km % 4) * 2, km * 2, km % 2
                if now(g, k):
                    row_max(g, k, 0)
                p = k - 1
                if p % TB in PROJ_AT and now(g, p, -TB):
                    low_part(g * 2 + p // TB + 1, (p // TB + 1) % 2, PROJ_AT.index(p % TB),
                             slot[SLOT[p, "proj"]])
                if j == 2 and now(g, k - j, 2 * QB):
                    add_y(g, kb)
                if now(g, k):
                    row_max(g, k, 1)
                if now(g, k, 1):
                    dve.wait_ge(exp_done, 2 * m + 2)
                    dve.reciprocal(l_inv[:, r:r + 2], l_sum[:, l:l + 2]).then_inc(recip_done, 1)
                    dve.tensor_scalar(l1_neg[:, e:e + 1], l_sum[:, l:l + 1], lam_neg, None, ALU.mult)\
                        .then_inc(recip_done, 1)
                    dve.wait_ge(recip_done, 2 * m + 2)
                    e2 = e2_buf[:, km % 4 * S:(km % 4 + 1) * S]
                    dve.tensor_scalar(e2, e2, l_inv[:, r + 1:r + 2], l1_neg[:, e:e + 1], ALU.mult, ALU.mult)\
                        .then_inc(scaled, 1)

            def norm_y(part):
                half = part % 2
                tiles = slice(half * TB, (half + 1) * TB)
                yb = y3[:, tiles, :]

                def over_tokens(v):
                    return v[:, tiles].unsqueeze(2).to_broadcast([P, TB, E])

                if part in (0, 1):
                    dve.wait_ge(y_evac, STEPS // QB)
                    dve.tensor_reduce(sum_x[:, tiles], yb, AX.X, ALU.add).then_inc(lny, 1)
                    if half:
                        dve.wait_ge(lny, 2)
                        dve.tensor_scalar(mean_x, sum_x, 1.0 / E, None, ALU.mult).then_inc(lny, 1)
                elif part in (2, 3):
                    dve.wait_ge(lny, 3)
                    dve.tensor_tensor(yb, yb, over_tokens(mean_x), ALU.subtract).then_inc(lny, 1)
                elif part in (4, 5):
                    dve.wait_ge(lny, 4 + half)
                    dve.tensor_tensor(y_sq[:, tiles, :], yb, yb, ALU.mult).then_inc(lny, 1)
                elif part in (6, 7):
                    dve.wait_ge(lny, 6 + half)
                    dve.tensor_reduce(sum_x[:, tiles], y_sq[:, tiles, :], AX.X, ALU.add).then_inc(lny, 1)
                    if half:
                        dve.wait_ge(lny, 9)
                        dve.tensor_scalar(var_x, sum_x, 1.0 / E, LN_EPS, ALU.mult, ALU.add).then_inc(lny, 1)

            def finish_y(part):
                if part == 0:
                    dve.wait_ge(lny_sqrt, 1)
                    inv_std(slice(0, NT), lny, 10)
                elif part <= 3 * B:
                    b, what = divmod(part - 1, 3)
                    tiles = slice(b * TB, (b + 1) * TB)
                    yb = y3[:, tiles, :]
                    other = (rstd_x[:, tiles].unsqueeze(2).to_broadcast([P, TB, E]),
                             gb_bc[:, 0:E].unsqueeze(1).to_broadcast([P, TB, E]), x3[:, tiles, :])[what]
                    dve.wait_ge(lny, 13 + part)
                    dve.tensor_tensor(yb, yb, other, (ALU.mult, ALU.mult, ALU.add)[what]).then_inc(lny, 1)

            def sum_up(b):
                dve.wait_ge(lny, 17 + 3 * b)
                dve.wait_ge(out_mm, (b + 1) * UNITS // B)
                for quad in range(2):
                    bank = ps[:, (6 + quad) * BANK:(7 + quad) * BANK]
                    part = y_acc[:, (2 * b + quad) * BANK:(2 * b + quad + 1) * BANK]
                    dve.tensor_tensor(part, part, bank, ALU.add).then_inc(f_out, 1)

            def network(u):
                if u < UNITS:
                    t = t_buf[u % Z_BUFS]
                    dve.wait_ge(z_done, u + 1)
                    dve.tensor_scalar(t, t, GELU_A, 1.0, ALU.mult, ALU.add).then_inc(cubic, 1)
                if GELU_LAG <= u < UNITS + GELU_LAG:
                    v = u - GELU_LAG
                    z, t = z_buf[v % Z_BUFS], t_buf[v % Z_BUFS]
                    dve.wait_ge(tanh_done, v + 1)
                    after(dve, out_mm, v - 3)
                    dve.scalar_tensor_tensor(out=hidden[v % 4], in0=t, scalar=1.0, in1=z,
                                             op0=ALU.add, op1=ALU.mult).then_inc(h_done, 1)

            def start_network(k):
                if k in (3, 4):
                    network(k - 3)

            attention(dve, step, QB + 3, start_network)
            for u in range(2, UNITS + OUT_LAG):
                if u == UNITS // B + OUT_LAG - 1:
                    sum_up(0)
                network(u)
                if u == 2:
                    norm_y(0)
                if u <= 8:
                    norm_y(u - 1)
                if u > SQRT_AT:
                    finish_y(u - SQRT_AT - 1)
            sum_up(1)


_INS = ["L0_attn_X", "L0_attn_Wq", "L0_attn_bq", "L0_attn_Wk", "L0_attn_bk", "L0_attn_Wv", "L0_attn_bv",
        "L0_attn_Wo", "L0_attn_bo", "L0_attn_gamma", "L0_attn_beta", "L0_attn_lam", "L0_ffn_alpha",
        "L0_ffn_w_gate", "L0_ffn_b_gate", "L0_ffn_W1m", "L0_ffn_b1m", "L0_ffn_W2m", "L0_ffn_b2m",
        "L0_ffn_W1e", "L0_ffn_b1e", "L0_ffn_W2e", "L0_ffn_b2e"]


def kernel(**inputs):
    import numpy as np
    import concourse.bacc as bacc
    from concourse.bass_utils import run_bass_kernel_spmd

    nc = bacc.Bacc("TRN2", target_bir_lowering=False, num_devices=1)
    arrays, args = {}, []
    for name in _INS:
        a = np.asarray(inputs[name])
        if name in ("L0_attn_bq", "L0_attn_bk"):
            a = a.T
        elif name in ("L0_ffn_b1m", "L0_ffn_b1e"):
            a = np.swapaxes(a.reshape(a.shape[:-1] + (HC, P)), -1, -2)
        a = np.ascontiguousarray(a)
        arrays[f"in_{name}"] = a
        args.append(nc.dram_tensor(f"in_{name}", a.shape, mybir.dt.from_np(a.dtype), kind="ExternalInput").ap())
    args.append(nc.dram_tensor("out", (B, S, E), F32, kind="ExternalOutput").ap())
    build(nc, *args)
    r = run_bass_kernel_spmd(nc, [arrays], core_ids=[0])
    return r.results[0]["out"]
```
